# Optimizing a Trainium2 kernel written in Bass

```python
import numpy as np
import jax
import jax.numpy as jnp

def _softmax(x, axis=-1):
    return jax.nn.softmax(x, axis=axis)

def _gelu(x):
    return jax.nn.gelu(x, approximate=True)

def _silu(x):
    return jax.nn.silu(x)

def _sigmoid(x):
    return jax.nn.sigmoid(x)

def _layernorm(x, axis=-1, eps=1e-05):
    m = jnp.mean(x, axis=axis, keepdims=True)
    v = jnp.var(x, axis=axis, keepdims=True)
    return (x - m) / jnp.sqrt(v + eps)

def _scatter_add(tgt, idx, src, axis=0):
    return tgt.at[idx].add(src)

def _segment_sum(src, seg, n):
    return jax.ops.segment_sum(src, seg, n)
kernel_name = 'mk_seq_postln_d1_jaxref_r8_6c5482'

def setup_inputs(seed: int=0):
    np.random.seed(seed)
    _w = jnp.asarray

    def _L0_attn_setup():
        import jax, jax.numpy as jnp
        import numpy as np
        B, T, C, R = (8, 128, 128, 64)
        EPS = 1e-05
        key = jax.random.key(seed)
        ks = jax.random.split(key, 8)
        x = jax.random.normal(ks[0], (B, T, C), dtype=jnp.float32)
        W_attn = jax.random.normal(ks[1], (3 * C, C), dtype=jnp.float32) * 0.02
        W_proj = jax.random.normal(ks[2], (C, C), dtype=jnp.float32) * 0.02
        lora_attn_A = jax.random.normal(ks[3], (C, R), dtype=jnp.float32) * 0.02
        lora_attn_B = jax.random.normal(ks[4], (R, 3 * C), dtype=jnp.float32) * 0.02
        lora_proj_A = jax.random.normal(ks[5], (C, R), dtype=jnp.float32) * 0.02
        lora_proj_B = jax.random.normal(ks[6], (R, C), dtype=jnp.float32) * 0.02
        bn_gamma = jnp.ones((3 * C,), dtype=jnp.float32)
        bn_beta = jnp.zeros((3 * C,), dtype=jnp.float32)
        return {'x': x, 'W_attn': W_attn, 'W_proj': W_proj, 'lora_attn_A': lora_attn_A, 'lora_attn_B': lora_attn_B, 'lora_proj_A': lora_proj_A, 'lora_proj_B': lora_proj_B, 'bn_gamma': bn_gamma, 'bn_beta': bn_beta}
    _L0_attn_in = _L0_attn_setup()

    def _L0_ffn_setup():
        import jax, jax.numpy as jnp
        import numpy as np
        B, S, D, E, H, K = (4, 256, 128, 8, 512, 2)
        EPS = 1e-06

        def _ln(x, scale, bias):
            m = jnp.mean(x, axis=-1, keepdims=True)
            v = jnp.mean(jnp.square(x - m), axis=-1, keepdims=True)
            return (x - m) * jax.lax.rsqrt(v + EPS) * scale + bias
        key = jax.random.key(seed)
        ks = jax.random.split(key, 4)
        s1 = 1.0 / np.sqrt(D)
        s2 = 1.0 / np.sqrt(H)
        return {'x': jax.random.normal(ks[0], (B, S, D), jnp.float32), 'router_ln_scale': jnp.ones((D,), jnp.float32), 'router_ln_bias': jnp.zeros((D,), jnp.float32), 'router_w': jax.random.normal(ks[1], (E, D), jnp.float32) * s1, 'router_b': jnp.zeros((E,), jnp.float32), 'expert_ln_scale': jnp.ones((E, D), jnp.float32), 'expert_ln_bias': jnp.zeros((E, D), jnp.float32), 'w1': jax.random.normal(ks[2], (E, H, D), jnp.float32) * s1, 'b1': jnp.zeros((E, H), jnp.float32), 'w2': jax.random.normal(ks[3], (E, D, H), jnp.float32) * s2, 'b2': jnp.zeros((E, D), jnp.float32)}
    _L0_ffn_in = _L0_ffn_setup()
    _d = {'L0_attn_x': _L0_attn_in['x'], 'L0_attn_W_attn': _L0_attn_in['W_attn'], 'L0_attn_W_proj': _L0_attn_in['W_proj'], 'L0_attn_lora_attn_A': _L0_attn_in['lora_attn_A'], 'L0_attn_lora_attn_B': _L0_attn_in['lora_attn_B'], 'L0_attn_lora_proj_A': _L0_attn_in['lora_proj_A'], 'L0_attn_lora_proj_B': _L0_attn_in['lora_proj_B'], 'L0_attn_bn_gamma': _L0_attn_in['bn_gamma'], 'L0_attn_bn_beta': _L0_attn_in['bn_beta'], 'L0_ffn_router_ln_scale': _L0_ffn_in['router_ln_scale'], 'L0_ffn_router_ln_bias': _L0_ffn_in['router_ln_bias'], 'L0_ffn_router_w': _L0_ffn_in['router_w'], 'L0_ffn_router_b': _L0_ffn_in['router_b'], 'L0_ffn_expert_ln_scale': _L0_ffn_in['expert_ln_scale'], 'L0_ffn_expert_ln_bias': _L0_ffn_in['expert_ln_bias'], 'L0_ffn_w1': _L0_ffn_in['w1'], 'L0_ffn_b1': _L0_ffn_in['b1'], 'L0_ffn_w2': _L0_ffn_in['w2'], 'L0_ffn_b2': _L0_ffn_in['b2']}
    _x0 = _d['L0_attn_x']
    _d['L0_attn_x'] = jax.random.normal(jax.random.fold_in(jax.random.key(seed), 1), (32, 256, 128), dtype=_x0.dtype)
    del _x0
    return _d

def reference(L0_attn_x, L0_attn_W_attn, L0_attn_W_proj, L0_attn_lora_attn_A, L0_attn_lora_attn_B, L0_attn_lora_proj_A, L0_attn_lora_proj_B, L0_attn_bn_gamma, L0_attn_bn_beta, L0_ffn_router_ln_scale, L0_ffn_router_ln_bias, L0_ffn_router_w, L0_ffn_router_b, L0_ffn_expert_ln_scale, L0_ffn_expert_ln_bias, L0_ffn_w1, L0_ffn_b1, L0_ffn_w2, L0_ffn_b2):

    def _L0_attn_ref(x, W_attn, W_proj, lora_attn_A, lora_attn_B, lora_proj_A, lora_proj_B, bn_gamma, bn_beta):
        import jax, jax.numpy as jnp
        import numpy as np
        B, T, C, R = (8, 128, 128, 64)
        EPS = 1e-05
        Bb, Tt, Cc = x.shape
        Wm_attn = W_attn + (lora_attn_A @ lora_attn_B).reshape(W_attn.shape)
        xa = jnp.einsum('btc,dc->btd', x, Wm_attn)
        mean = xa.mean(axis=(0, 1))
        var = xa.var(axis=(0, 1))
        xa = (xa - mean) * jax.lax.rsqrt(var + EPS) * bn_gamma + bn_beta
        q, k, v = jnp.split(xa, 3, axis=-1)
        scale = 1.0 / jnp.sqrt(jnp.asarray(Cc, dtype=x.dtype))
        att = jnp.einsum('btc,bsc->bts', q, k) * scale
        causal = jnp.tril(jnp.ones((Tt, Tt), dtype=bool))
        att = jnp.where(causal[None, :, :], att, -jnp.inf)
        att = jax.nn.softmax(att, axis=-1)
        y = jnp.einsum('bts,bsc->btc', att, v)
        y = jnp.einsum('btc,dc->btd', y, W_proj)
        Wm_proj = W_proj + (lora_proj_A @ lora_proj_B).reshape(W_proj.shape)
        y = jnp.einsum('btc,dc->btd', y, Wm_proj)
        return y

    def _L0_ffn_ref(x, router_ln_scale, router_ln_bias, router_w, router_b, expert_ln_scale, expert_ln_bias, w1, b1, w2, b2):
        import jax, jax.numpy as jnp
        import numpy as np
        B, S, D, E, H, K = (4, 256, 128, 8, 512, 2)
        EPS = 1e-06

        def _ln(x, scale, bias):
            m = jnp.mean(x, axis=-1, keepdims=True)
            v = jnp.mean(jnp.square(x - m), axis=-1, keepdims=True)
            return (x - m) * jax.lax.rsqrt(v + EPS) * scale + bias
        orig_shape = x.shape
        xf = x.reshape(-1, D)
        T = xf.shape[0]
        logits = _ln(xf, router_ln_scale, router_ln_bias) @ router_w.T + router_b
        probs = jax.nn.softmax(logits, axis=-1)
        topw, topi = jax.lax.top_k(probs, K)
        topw = topw / jnp.sum(topw, axis=-1, keepdims=True)
        gates = jnp.zeros((T, E), xf.dtype).at[jnp.arange(T)[:, None], topi].set(topw)

        def expert(ls, lb, W1, B1, W2, B2):
            h = jax.nn.gelu(_ln(xf, ls, lb) @ W1.T + B1, approximate=False)
            return h @ W2.T + B2
        ys = jax.vmap(expert)(expert_ln_scale, expert_ln_bias, w1, b1, w2, b2)
        out = jnp.einsum('te,etd->td', gates, ys)
        return out.reshape(orig_shape)
    x = L0_attn_x
    x = _layernorm(x + _L0_attn_ref(x, L0_attn_W_attn, L0_attn_W_proj, L0_attn_lora_attn_A, L0_attn_lora_attn_B, L0_attn_lora_proj_A, L0_attn_lora_proj_B, L0_attn_bn_gamma, L0_attn_bn_beta), axis=-1)
    x = _layernorm(x + _L0_ffn_ref(x, L0_ffn_router_ln_scale, L0_ffn_router_ln_bias, L0_ffn_router_w, L0_ffn_router_b, L0_ffn_expert_ln_scale, L0_ffn_expert_ln_bias, L0_ffn_w1, L0_ffn_b1, L0_ffn_w2, L0_ffn_b2), axis=-1)
    return x

_drawn_inputs = setup_inputs


def setup_inputs(seed=0):
    import zlib

    import numpy as np

    out = dict(_drawn_inputs(seed))
    spreads = {'L0_attn_bn_gamma': (1.0, 0.6),
     'L0_attn_bn_beta': (0.0, 0.1),
     'L0_ffn_router_ln_scale': (1.0, 0.2),
     'L0_ffn_router_ln_bias': (0.0, 0.1),
     'L0_ffn_router_b': (0.0, 0.1),
     'L0_ffn_expert_ln_scale': (1.0, 0.2),
     'L0_ffn_expert_ln_bias': (0.0, 0.1),
     'L0_ffn_b1': (0.0, 0.1),
     'L0_ffn_b2': (0.0, 0.1)}
    factors = {'L0_attn_lora_attn_A': 3.675,
     'L0_attn_lora_attn_B': 2.988,
     'L0_attn_lora_proj_A': 4.241,
     'L0_attn_lora_proj_B': 4.139}
    for name, (base, spread) in spreads.items():
        noise = np.random.default_rng([zlib.crc32(name.encode()), seed]).standard_normal(out[name].shape)
        drawn = base * np.exp(spread * noise) if base else spread * noise
        out[name] = jnp.asarray(drawn.astype(out[name].dtype))
    for name, factor in factors.items():
        out[name] = (out[name] * factor).astype(out[name].dtype)
    return out
```

```python
from contextlib import ExitStack

import concourse.bass as bass
from concourse import mybir

F32 = mybir.dt.float32
BF16 = mybir.dt.bfloat16
I32 = mybir.dt.int32
U32 = mybir.dt.uint32
ALU = mybir.AluOpType
ACT = mybir.ActivationFunctionType
AXX = mybir.AxisListType.X

P = 128
MASKED = -1e30
EPS_BN = 1e-5
EPS_POST = 1e-5
EPS_FFN = 1e-6
RSQRT_GUESS = float(0x5F3759DF)
RSQRT_OPS = 14


class Progress:

    def __init__(self, eng, sem):
        self.eng, self.sem, self.base, self.n = eng, sem, 0, 0

    def did(self, ins):
        ins.then_inc(self.sem, 1)
        self.n += 1

    def settle(self):
        self.eng.wait_ge(self.sem, self.base + self.n)


def wait(eng, sem, value):
    if isinstance(value, int) and value <= 0:
        return
    eng.wait_ge(sem, value)


def run_steps(eng, step, total, unroll, front, back, progress=None, per_step=0):
    loops = (total - front - back) // unroll
    for k in range(front):
        step(k, k % unroll, k // unroll, k)
    if loops:
        start = progress.n if progress else 0
        with eng.Fori(0, loops) as i:
            if progress:
                progress.base = eng.snap(i * (unroll * per_step))
            for j in range(front, front + unroll):
                step(eng.snap(i * unroll + j), j % unroll, eng.snap(i + j // unroll), None)
            if progress:
                assert progress.n - start == unroll * per_step, (progress.n - start, unroll * per_step)
        if progress:
            progress.base, progress.n = 0, start + loops * unroll * per_step
    for k in range(front + loops * unroll, total):
        step(k, k % unroll, k // unroll, k)


def build(nc, x, w_attn, w_proj, la_a, la_b, lp_a, lp_b, gamma, beta, r_ls, r_lb, r_w, r_b,
          e_ls, e_lb, w1, b1, w2, b2, out):
    NB, T, C = x.shape
    E, H, _ = w1.shape
    R = la_a.shape[1]
    HC = H // P
    NTOK = NB * T
    NT = NTOK // P
    TPB = T // P
    CAP = NTOK + P
    DUMMY = E * CAP
    NTILE = 2 * NT + E - 1 + 1
    NTILE += NTILE % 2
    assert C == P and TPB == 2

    queue = nc.dram_tensor("queue", [DUMMY + E * P, P], F32, kind="Internal").ap()
    yrows = nc.dram_tensor("yrows", [NTILE * P, P], F32, kind="Internal").ap()

    with ExitStack() as ctx:
        def sb(name, shape, dt=F32):
            return ctx.enter_context(nc.sbuf_tensor(name, shape, dt))

        def sem(name):
            return ctx.enter_context(nc.semaphore(name))

        bank = [ctx.enter_context(nc.psum_tensor(f"bank{i}", [P, 512], F32)) for i in range(8)]

        xT = sb("xT", [P, NTOK])
        x_all = sb("x_all", [P, NT, P])
        w1T = sb("w1T", [P, E, H])
        w2T = sb("w2T", [P, E, HC, P])
        b2_bc = sb("b2_bc", [P, E, P])
        oh_all = sb("oh_all", [P, NT, 2, E])
        pos_all = sb("pos_all", [P, NT, 2])
        lg_all = sb("lg_all", [P, NT, 2])
        gates = sb("gates", [P, NT, 2])
        ypos = sb("ypos", [P, NT, 2], I32)

        late_used = [0]

        def late(shape):
            n, at = 1, late_used[0]
            for d in shape[1:]:
                n *= d
            late_used[0] += n
            assert late_used[0] <= NTOK
            names = "abcd"[:len(shape) - 1]
            return xT[:, at:at + n].rearrange(f"p ({' '.join(names)}) -> p {' '.join(names)}",
                                              **dict(zip(names, shape[1:])))

        ident = sb("ident", [P, P])
        ident_b = sb("ident_b", [P, P], BF16)
        mask_b = sb("mask_b", [P, P], BF16)
        before = sb("before", [P, P])
        ones = sb("ones", [P, P])
        ones_b = sb("ones_b", [P, P], BF16)
        zeros = sb("zeros", [P, P])
        inv_c = sb("inv_c", [1, P])
        iota_e = sb("iota_e", [P, E])
        part = sb("part", [P, 1])
        one_col = sb("one_col", [P, 1])

        s_const, s_par, s_go = sem("s_const"), sem("s_par"), sem("s_go")
        s_pe, s_dve, s_act, s_pool = sem("s_pe"), sem("s_dve"), sem("s_act"), sem("s_pool")

        CH, RING = 4, 4
        NCH = NT // CH
        xin = sb("xin", [P, RING, CH, 132])
        s_xin = [sem(f"s_xin{i}") for i in range(RING)]
        s_t1, s_cp1 = sem("s_t1"), sem("s_cp1")
        s_ev = [sem("s_ev_act"), sem("s_ev_dve")]
        x_chunks = x.rearrange("b t c -> (b t) c").rearrange("(n j p) c -> n p j c", j=CH, p=P)

        wa = sb("wa", [P, 3, P])
        wp = sb("wp", [P, P])
        aA, aB = sb("aA", [P, R]), sb("aB", [R, 3 * P])
        pA, pB = sb("pA", [P, R]), sb("pB", [R, P])
        gb = sb("gb", [P, 2, 3])
        rls, rlb = sb("rls", [P, 1]), sb("rlb", [P, 1])
        els, elb = sb("els", [P, E]), sb("elb", [P, E])
        rwT, rb = sb("rwT", [P, E]), sb("rb", [1, E])
        aAT, pAT = sb("aAT", [R, P]), sb("pAT", [R, P])
        wm = sb("wm", [P, 3, P])
        wmT = sb("wmT", [P, 3 * P])
        wn = sb("wn", [P, 3, P])
        cov = sb("cov", [P, P + 1])
        mu_row, nmu_row = sb("mu_row", [1, P]), sb("nmu_row", [1, P])
        proj = sb("proj", [P, 3, P + 1])
        scr3 = sb("scr3", [P, 3, P])
        bn = sb("bn", [P, 4, 3])
        bn_i = sb("bn_i", [P, 3], I32)
        wpmT = sb("wpmT", [P, P])
        wp2T = sb("wp2T", [P, P])
        tv_bc = sb("tv_bc", [P, P])
        MT = sb("MT", [P, P])
        u_z = sb("u_z", [P, 1])
        wvvT = sb("wvvT", [P, P])
        cv = sb("cv", [P, P])
        rl_bc = sb("rl_bc", [P, P])
        rl_d = sb("rl_d", [P, 1])
        RW = sb("RW", [P, E])

        w1n = sb("w1n", [P, 2, HC, P])
        w2n = sb("w2n", [P, 2, H])
        b1r = sb("b1r", [1, 2, H])
        w1raw = sb("w1raw", [P, 2, H])
        l_bc = sb("l_bc", [P, 2, P])
        el_d = sb("el_d", [P, E])
        s_w = [sem("s_w0"), sem("s_w1")]
        s_w1t, s_w2t, s_w1c, s_w2c, s_lbc, s_w1f, s_w1o = [sem(n) for n in (
            "s_w1t", "s_w2t", "s_w1c", "s_w2c", "s_lbc", "s_w1f", "s_w1o")]

        U = 4
        xTs = sb("xTs", [P, 2, T])
        zT = sb("zT", [P, 2, T])
        vs = sb("vs", [P, 2, TPB, P])
        nmax, rsum, rinv = sb("nmax", [P, 2, TPB]), sb("rsum", [P, 2, TPB]), sb("rinv", [P, TPB])
        pr = sb("pr", [P, 2, 3, P])
        prT = sb("prT", [P, 2, 3, P])
        x1 = sb("x1", [P, TPB, P])
        st6, mv = sb("st6", [P, TPB, 6]), sb("mv", [P, TPB, 2])
        vv = sb("vv", [P, 2, 2, TPB])
        lnv = sb("lnv", [P, 2, 2, TPB])
        rr = sb("rr", [P, 2, 2, TPB])
        xh = sb("xh", [P, U, TPB, P])
        xhT = sb("xhT", [P, 2, TPB, P])
        mx8 = sb("mx8", [P, TPB, 8])
        ix8 = sb("ix8", [P, TPB, 8], U32)
        m_sum = sb("m_sum", [P, 2, TPB, E])
        run = sb("run", [P, 2, TPB, E])
        ohc = sb("ohc", [P, TPB, 2, E])
        ohr = sb("ohr", [P, TPB, 2, E])
        posf = sb("posf", [P, TPB, 2])
        pos_i = sb("pos_i", [P, U, TPB, 2], I32)
        (s_xts, s_z, s_v, s_zs, s_vs, s_sc, s_mx, s_p, s_pt, s_pts, s_y, s_xh, s_xht, s_xhts,
         s_lg, s_oh, s_rk, s_pos, s_vv, s_ln, s_rr) = [sem(n) for n in (
            "s_xts", "s_z", "s_v", "s_zs", "s_vs", "s_sc", "s_mx", "s_p", "s_pt", "s_pts", "s_y", "s_xh",
            "s_xht", "s_xhts", "s_lg", "s_oh", "s_rk", "s_pos", "s_vv", "s_ln", "s_rr")]
        s_scat = [sem(f"s_scat{i}") for i in range(U)]

        cnt = sb("cnt", [P, E])
        tiles, incl, tb0 = sb("tiles", [P, E]), sb("incl", [P, E]), sb("tb0", [P, E])
        ebase = sb("ebase", [P, E])
        shift = sb("shift", [P, E + 1])
        e_iota = sb("e_iota", [1, E + 1])
        j_iota = sb("j_iota", [1, NTILE])
        cmp = sb("cmp", [1, NTILE, E])
        kP_iota = sb("kP_iota", [P, NT])
        full = sb("full", [P, E, NT])
        ej = sb("ej", [1, NTILE])
        cmp9 = sb("cmp9", [1, NTILE, E + 1])
        rowf = sb("rowf", [1, NTILE])
        tab_row, tab_e = sb("tab_row", [1, NTILE], I32), sb("tab_e", [1, NTILE], I32)
        padp = sb("padp", [P, E], I32)
        padf = sb("padf", [P, E])
        ohs = late([P, NT * 2, E])
        yf = sb("yf", [P, NT * 2])
        gd = sb("gd", [P, NT])
        s_tot, s_tab, s_pad, s_padd, s_zero, s_gd, s_ge, s_gates = [sem(n) for n in (
            "s_tot", "s_tab", "s_pad", "s_padd", "s_zero", "s_gd", "s_ge", "s_gates")]

        XR = 4
        xg = late([P, XR, P])
        xgT = late([P, 2, P])
        w1c = late([P, 2, H])
        hs = late([P, 2, HC, P])
        ysb = late([P, XR, P])
        s_xg = [sem(f"s_xg{i}") for i in range(XR)]
        s_yo = [sem(f"s_yo{i}") for i in range(XR)]
        s_gt, s_gts, s_w1s, s_h, s_hs, s_yy, s_ys = [sem(n) for n in (
            "s_gt", "s_gts", "s_w1s", "s_h", "s_hs", "s_yy", "s_ys")]

        gy = late([P, 2, TPB, 2, P])
        yidx = sb("yidx", [P, 2, TPB, 2], I32)
        acc = late([P, 2, TPB, P])
        osb = late([P, 4, TPB, P])
        st7, mv7, r7 = sb("st7", [P, TPB, 6]), sb("mv7", [P, TPB, 2]), sb("r7", [P, TPB])
        v7, t7, t7i = sb("v7", [P, TPB]), sb("t7", [P, TPB]), sb("t7i", [P, TPB], I32)
        s_yi, s_comb, s_os = sem("s_yi"), sem("s_comb"), sem("s_os")
        s_gy = [sem("s_gy0"), sem("s_gy1")]
        s_out = [sem(f"s_out{i}") for i in range(4)]

        N_PARAM = 14

        s_own_dve, s_own_pool = sem("s_own_dve"), sem("s_own_pool")

        def own_wait(eng, s_own):
            eng.sem_inc(s_own, 1)

        out_v = out.rearrange("b (j p) c -> b p j c", p=P)

        block = ctx.enter_context(nc.Block())

        @block.sync
        def _(sp):
            def load_chunk(c, slot):
                sp.dma_start(xin[:, slot, :, 0:P], x_chunks[c]).then_inc(s_xin[slot], 16)

            for c in range(RING):
                load_chunk(c, c)
            with nc.allow_non_contiguous_dma(reason="small parameters, transposed"):
                for dst, src in ((wa[:], w_attn.rearrange("(i a) c -> i a c", a=3)), (wp[:], w_proj),
                                 (aA[:], la_a), (aB[:], la_b), (pA[:], lp_a), (pB[:], lp_b),
                                 (gb[:, 0, :], gamma.rearrange("(a p) -> p a", p=P)),
                                 (gb[:, 1, :], beta.rearrange("(a p) -> p a", p=P)),
                                 (rls[:], r_ls.unsqueeze(1)), (rlb[:], r_lb.unsqueeze(1)),
                                 (rb[:], r_b.unsqueeze(0)), (rwT[:], r_w.rearrange("e d -> d e")),
                                 (els[:], e_ls.rearrange("e d -> d e")), (elb[:], e_lb.rearrange("e d -> d e"))):
                    sp.dma_start(dst, src).then_inc(s_par, 16)
            sp.dma_start(b2_bc[:], b2.partition_broadcast(P)).then_inc(s_go, 16)
            with sp.Fori(1, NCH // RING) as i:
                for j in range(RING):
                    sp.wait_ge(s_t1, i * RING + (j - RING + 1))
                    sp.wait_ge(s_cp1, i * RING + (j - RING + 1))
                    load_chunk(i * RING + j, j)
            wait(sp, s_const, 1)
            sp.dma_start(queue[DUMMY:DUMMY + E * P, :].rearrange("(a p) c -> p a c", p=P),
                         zeros[:, :].unsqueeze(1).to_broadcast([P, E, P])).then_inc(s_zero, 16)

            def load_expert(e, slot):
                wait(sp, s_w2t, e - 1)
                wait(sp, s_w1f, e - 1)
                sp.dma_start(w1n[:, slot], w1[e].rearrange("(k p) d -> p k d", p=P)).then_inc(s_w[slot], 16)
                sp.dma_start(w2n[:, slot], w2[e]).then_inc(s_w[slot], 16)
                sp.dma_start(b1r[:, slot], b1[e].unsqueeze(0)).then_inc(s_w[slot], 16)
            for e in range(2):
                load_expert(e, e)
            with sp.Fori(1, E // 2) as i:
                for j in range(2):
                    load_expert(sp.snap(i * 2 + j), j)

            for q in range(U):
                sp.wait_ge(s_scat[q], 16 * 2 * TPB * (NB // U))
            sp.wait_ge(s_padd, 16 * E)
            sp.wait_ge(s_zero, 16)
            sp.wait_ge(s_tab, 1)

            def load_rows(j, slot):
                wait(sp, s_gt, j - XR + 1)
                row = sp.value_load(tab_row[0:1, bass.ds(j, 1)], min_val=0, max_val=DUMMY + (E - 1) * P)
                sp.dma_start(xg[:, slot], queue[bass.ds(row, P), :]).then_inc(s_xg[slot], 16)

            def ffn_step(k, slot, use, known):
                if known is None or known < NTILE:
                    load_rows(k, slot)
                if known is None or known >= 4:
                    j = k - 4
                    wait(sp, s_ys, j + 1)
                    sp.dma_start(yrows[bass.ds(j * P, P), :], ysb[:, slot]).then_inc(s_yo[slot], 16)
            run_steps(sp, ffn_step, NTILE + 4, XR, 4, 4)

            def store_step(b, slot, use, known):
                wait(sp, s_os, b + 1)
                sp.dma_start(out_v[b], osb[:, slot]).then_inc(s_out[slot], 16)
            run_steps(sp, store_step, NB, 4, 0, 0)
            for q in range(4):
                sp.wait_ge(s_out[q], 16 * (NB // 4))

        @block.gpsimd
        def _(pool):
            pg = Progress(pool, s_pool)
            pg.did(pool.memset(ones[:], 1.0))
            pg.did(pool.memset(ones_b[:], 1.0))
            pg.did(pool.memset(zeros[:], 0.0))
            pg.did(pool.memset(inv_c[:], 1.0 / C))
            pg.did(pool.memset(one_col[:], 1.0))
            for s in range(RING):
                pg.did(pool.memset(xin[:, s, :, P:P + 1], 1.0))
            pg.did(pool.memset(mask_b[:], 0.0))
            pg.did(pool.iota(iota_e[:], [[1, E]], base=0, channel_multiplier=0, allow_small_or_imprecise_dtypes=True))
            pg.did(pool.iota(e_iota[:], [[1, E + 1]], base=0, channel_multiplier=0, allow_small_or_imprecise_dtypes=True))
            pg.did(pool.iota(j_iota[:], [[1, NTILE]], base=0, channel_multiplier=0, allow_small_or_imprecise_dtypes=True))
            pg.did(pool.iota(kP_iota[:], [[P, NT]], base=0, channel_multiplier=0, allow_small_or_imprecise_dtypes=True))
            pg.did(pool.iota(part[:], [[0, 1]], base=0, channel_multiplier=1, allow_small_or_imprecise_dtypes=True))
            pg.did(pool.iota(ebase[:], [[CAP, E]], base=0, channel_multiplier=0, allow_small_or_imprecise_dtypes=True))
            pg.settle()
            pg.did(pool.affine_select(out=ident[:], in_=ones[:], pattern=[[-1, P]], compare_op=ALU.is_equal,
                                      fill=0.0, base=0, channel_multiplier=1))
            pg.did(pool.affine_select(out=ident_b[:], in_=ones_b[:], pattern=[[-1, P]], compare_op=ALU.is_equal,
                                      fill=0.0, base=0, channel_multiplier=1))
            pg.did(pool.affine_select(out=mask_b[:], in_=mask_b[:], pattern=[[-1, P]], compare_op=ALU.is_ge,
                                      fill=MASKED, base=0, channel_multiplier=1))
            pg.did(pool.affine_select(out=before[:], in_=ones[:], pattern=[[1, P]], compare_op=ALU.is_gt,
                                      fill=0.0, base=0, channel_multiplier=-1))
            pg.settle()
            pool.sem_inc(s_const, 1)
            with pool.Fori(0, NCH // RING) as i:
                for j in range(RING):
                    pool.wait_ge(s_xin[j], i * 16 + 16)
                    pool.tensor_copy(x_all[:, bass.ds(i * (RING * CH) + j * CH, CH), :],
                                     xin[:, j, :, 0:P]).then_inc(s_cp1, 1)
            pool.wait_ge(s_ev[0], NCH // 2)
            pool.wait_ge(s_ev[1], NCH // 2)

            def attend_step(k, q, use, known):
                s = q % 2
                if known is None or known < NB:
                    wait(pool, s_sc, k - 1)
                    pool.tensor_copy(xTs[:, s, :], xT[:, bass.ds(k * T, T)]).then_inc(s_xts, 1)
                if known is None or known >= 3:
                    b, bq = k - 3, (q - 3) % U
                    wait(pool, s_pos, b + 1)
                    own_wait(pool, s_own_pool)
                    for t in range(TPB):
                        for c in range(2):
                            pool.indirect_dma_start(
                                out=queue, out_offset=bass.IndirectOffsetOnAxis(pos_i[:, bq, t, c:c + 1], 0),
                                in_=xh[:, bq, t, :], in_offset=None).then_inc(s_scat[bq], 16)
            run_steps(pool, attend_step, NB + 3, U, 3, 4)
            pool.wait_ge(s_pad, 1)
            for e in range(E):
                pool.indirect_dma_start(out=queue, out_offset=bass.IndirectOffsetOnAxis(padp[:, e:e + 1], 0),
                                        in_=zeros[:], in_offset=None).then_inc(s_padd, 16)
            for q in range(XR):
                n = len(range(q, NTILE, XR))
                pool.wait_ge(s_yo[q], 16 * n)

            def gather_step(b, q, use, known):
                s = q % 2
                wait(pool, s_comb, b - 1)
                pool.tensor_copy(yidx[:, s], ypos[:, bass.ds(b * TPB, TPB), :]).then_inc(s_yi, 1)
                wait(pool, s_yi, b + 1)
                own_wait(pool, s_own_pool)
                for t in range(TPB):
                    for c in range(2):
                        pool.indirect_dma_start(
                            out=gy[:, s, t, c, :], out_offset=None, in_=yrows,
                            in_offset=bass.IndirectOffsetOnAxis(yidx[:, s, t, c:c + 1], 0)).then_inc(s_gy[s], 16)
            run_steps(pool, gather_step, NB, 2, 2, 0)

        s_fold_pe, s_fold_dve = sem("s_fold_pe"), sem("s_fold_dve")

        @block.tensor
        def _(pe):
            mm, tr = pe.matmul, pe.transpose
            pe.wait_ge(s_const, 1)
            gram = bank[7][:, 0:P + 1]

            def gram_zero(start):
                return mm(gram, zeros[:], xin[:, 0, 0, 0:P + 1], start=start, stop=not start)

            pe.wait_ge(s_xin[0], 16)
            gram_zero(True)

            def chunk_step(k, q, use, known):
                pe.wait_ge(s_xin[q], use * 16 + 16)
                wait(pe, s_ev[q % 2], use * 2 + q // 2)
                for t in range(CH):
                    tr(bank[q % 2][:, t * P:(t + 1) * P], xin[:, q, t, 0:P], ident[:])
                for t in range(CH):
                    last = mm(gram, xin[:, q, t, 0:P], xin[:, q, t, 0:P + 1], start=False, stop=False)
                last.then_inc(s_t1, 1)
            run_steps(pe, chunk_step, NCH, RING, RING, 0)
            gram_zero(False)

            def round_opens(r):
                wait(pe, s_fold_dve, r)

            pe.wait_ge(s_par, 16 * N_PARAM)
            for h in range(2):
                pe.wait_ge(s_ev[h], NCH // 2)
            tr(bank[0][0:R, 0:P], aA[:], ident[:])
            tr(bank[0][0:R, P:2 * P], pA[:], ident[:]).then_inc(s_fold_pe, 1)
            round_opens(1)
            mm(bank[1][:, 0:3 * P], aAT[:], aB[:], start=True, stop=True)
            mm(bank[2][:, 0:P], wp[:], ident[:], start=True, stop=False)
            mm(bank[2][:, 0:P], pB[:], pAT[:], start=False, stop=True)
            mm(bank[3][0:1, 0:P], cov[:, P:P + 1], ident[:], start=True, stop=True).then_inc(s_fold_pe, 1)
            round_opens(2)
            for a in range(3):
                tr(bank[0][:, a * P:(a + 1) * P], wm[:, a, :], ident[:])
            mm(bank[3][:, P:2 * P], nmu_row[:], mu_row[:], start=True, stop=True)
            mm(bank[2][:, P:2 * P], wp[:], wpmT[:], start=True, stop=True).then_inc(s_fold_pe, 1)
            round_opens(3)
            for g in range(3):
                tr(bank[0][:, g * P:(g + 1) * P], wmT[:, g * P:(g + 1) * P], ident[:])
            for g in range(3):
                last = mm(bank[1][:, g * (P + 1):(g + 1) * (P + 1)], wmT[:, g * P:(g + 1) * P], cov[:],
                          start=True, stop=True)
            last.then_inc(s_fold_pe, 1)
            round_opens(4)
            mm(bank[2][:, 0:P], wn[:, 0, :], wn[:, 1, :], start=True, stop=True)
            mm(bank[2][:, P:P + 1], wn[:, 1, :], bn[:, 2, 0:1], start=True, stop=True)
            mm(bank[3][:, 0:P], wn[:, 2, :], wp2T[:], start=True, stop=True)
            mm(bank[3][:, P:2 * P], tv_bc[:], wp2T[:], start=True, stop=True)
            mm(bank[3][:, 2 * P:2 * P + E], rl_bc[:], rwT[:], start=True, stop=False)
            mm(bank[3][:, 2 * P:2 * P + E], inv_c[:], rb[:], start=False, stop=True).then_inc(s_fold_pe, 1)
            round_opens(5)

            def expert_step(e, q, use, known):
                pe.wait_ge(s_w[q], use * 48 + 48)
                wait(pe, s_w1c, e - 1)
                wait(pe, s_w2c, e - 1)
                for h in range(HC):
                    last = tr(bank[q][:, h * P:(h + 1) * P], w1n[:, q, h, :], ident[:])
                last.then_inc(s_w1t, 1)
                for h in range(HC):
                    last = tr(bank[2 + q][:, h * P:(h + 1) * P], w2n[:, q, h * P:(h + 1) * P], ident[:])
                last.then_inc(s_w2t, 1)
                pe.wait_ge(s_w1c, e + 1)
                pe.wait_ge(s_lbc, e + 1)
                wait(pe, s_w1o, e - 1)
                mm(bank[4 + q][:], l_bc[:, q, :], w1raw[:, q, :], start=True, stop=False)
                mm(bank[4 + q][:], inv_c[:], b1r[:, q, :], start=False, stop=True).then_inc(s_w1f, 1)
            run_steps(pe, expert_step, E, 2, 2, 0)
            pe.wait_ge(s_w2c, E)
            pe.wait_ge(s_w1o, E)

            def attend_step(k, q, use, known):
                has = [known is None or 0 <= known - d < NB for d in range(3)]
                if has[2]:
                    b, s = k - 2, q % 2
                    pe.wait_ge(s_xh, b + 1)
                    wait(pe, s_xhts, b)
                    for t in range(TPB):
                        last = tr(bank[6][:, t * P:(t + 1) * P], xh[:, (q - 2) % U, t, :], ident[:])
                    last.then_inc(s_xht, 1)
                if has[0]:
                    b, s = k, q % 2
                    pe.wait_ge(s_xts, b + 1)
                    wait(pe, s_zs, b)
                    mm(bank[0][:, 0:T], MT[:], xTs[:, s, :], start=True, stop=True).then_inc(s_z, 1)
                    wait(pe, s_vs, b)
                    for t in range(TPB):
                        last = mm(bank[1][:, t * P:(t + 1) * P], xTs[:, s, t * P:(t + 1) * P], wvvT[:],
                                  start=True, stop=True)
                    last.then_inc(s_v, 1)
                if has[2]:
                    b, s = k - 2, q % 2
                    pe.wait_ge(s_xhts, b + 1)
                    wait(pe, s_pos, b)
                    for t in range(TPB):
                        last = mm(bank[7][:, t * E:(t + 1) * E], xhT[:, s, t, :], RW[:], start=True, stop=True)
                    last.then_inc(s_lg, 1)
                if has[1]:
                    b, s = k - 1, (q - 1) % 2
                    pe.wait_ge(s_p, b + 1)
                    wait(pe, s_pts, b)
                    for n in range(3):
                        last = tr(bank[4][:, n * P:(n + 1) * P], pr[:, s, n, :], ident[:])
                    last.then_inc(s_pt, 1)
                if has[0]:
                    b, s = k, q % 2
                    pe.wait_ge(s_zs, b + 1)
                    wait(pe, s_p, b - 1)
                    sc = bank[2 + s]
                    mm(sc[:, 0:P], ident_b[:], mask_b[:], start=True, stop=False)
                    mm(sc[:, 0:P], zT[:, s, 0:P], xTs[:, s, 0:P], start=False, stop=True)
                    mm(sc[:, P:2 * P], zT[:, s, P:T], xTs[:, s, 0:P], start=True, stop=True)
                    mm(sc[:, 2 * P:3 * P], ident_b[:], mask_b[:], start=True, stop=False)
                    mm(sc[:, 2 * P:3 * P], zT[:, s, P:T], xTs[:, s, P:T], start=False,
                       stop=True).then_inc(s_sc, 1)
                if has[1]:
                    b, s = k - 1, (q - 1) % 2
                    pe.wait_ge(s_pts, b + 1)
                    pe.wait_ge(s_vs, b + 1)
                    wait(pe, s_vv, b)
                    mm(bank[5][:, 0:P], prT[:, s, 0, :], vs[:, s, 0, :], start=True, stop=True)
                    mm(bank[5][:, P:T], prT[:, s, 1, :], vs[:, s, 0, :], start=True, stop=False)
                    mm(bank[5][:, P:T], prT[:, s, 2, :], vs[:, s, 1, :], start=False, stop=True).then_inc(s_y, 1)
                if has[2]:
                    b, s = k - 2, q % 2
                    pe.wait_ge(s_oh, b + 1)
                    for t in range(TPB):
                        o = bank[7][:, (TPB + t) * E:(TPB + t + 1) * E]
                        mm(o, before[:], m_sum[:, s, t, :], start=True, stop=False)
                        last = mm(o, ones[:], run[:, s, t, :], start=False, stop=True)
                    last.then_inc(s_rk, 1)
            run_steps(pe, attend_step, NB + 2, U, 4, 2)

            pe.wait_ge(s_pos, NB)
            mm(bank[0][:, 0:E], ones[:], run[:, NB % 2, 0, :], start=True, stop=True).then_inc(s_tot, 1)

            pe.wait_ge(s_tab, 1)

            def ffn_step(k, q, use, known):
                if known is None or known < NTILE:
                    pe.wait_ge(s_xg[q], use * 16 + 16)
                    wait(pe, s_gts, k - 1)
                    tr(bank[q % 2][:, 0:P], xg[:, q, :], ident[:]).then_inc(s_gt, 1)
                if known is None or 0 <= known - 1 < NTILE:
                    j, s = k - 1, (q - 1) % 2
                    pe.wait_ge(s_gts, j + 1)
                    pe.wait_ge(s_w1s, j + 1)
                    wait(pe, s_hs, j - 1)
                    for h in range(HC):
                        last = mm(bank[2 + s][:, h * P:(h + 1) * P], w1c[:, s, h * P:(h + 1) * P], xgT[:, s, :],
                                  start=True, stop=True)
                    last.then_inc(s_h, 1)
                if known is None or 0 <= known - 2 < NTILE:
                    j, s = k - 2, q % 2
                    e = pe.value_load(tab_e[0:1, bass.ds(j, 1)], min_val=0, max_val=E - 1)
                    pe.wait_ge(s_hs, j + 1)
                    wait(pe, s_ys, j - 1)
                    for h in range(HC):
                        last = mm(bank[4 + s][:, 0:P], hs[:, s, h, :],
                                  w2T[:, bass.ds(e, 1), h, :].rearrange("p a d -> p (a d)"),
                                  start=(h == 0), stop=(h == HC - 1))
                    last.then_inc(s_yy, 1)
            run_steps(pe, ffn_step, NTILE + 2, XR, 4, 2)

        @block.scalar
        def _(act):
            def cp(out_, in_, bias=0.0):
                return act.activation(out_, in_, ACT.Identity, bias=bias)

            act.wait_ge(s_const, 1)
            with act.Fori(0, NCH // 2) as i:
                act.wait_ge(s_t1, i * 2 + 1)
                cp(xT[:, bass.ds(i * (2 * CH * P), CH * P)], bank[0][:]).then_inc(s_ev[0], 1)

            def expert_step(e, q, use, known):
                act.wait_ge(s_w1t, e + 1)
                wait(act, s_w1o, e - 1)
                cp(w1raw[:, q, :], bank[q][:]).then_inc(s_w1c, 1)
                act.wait_ge(s_w2t, e + 1)
                cp(w2T[:, bass.ds(e, 1), :, :].rearrange("p a h d -> p (a h d)"), bank[2 + q][:]).then_inc(s_w2c, 1)
            run_steps(act, expert_step, E, 2, 2, 0)

            def attend_step(k, q, use, known):
                has = [known is None or 0 <= known - d < NB for d in range(3)]
                if has[2]:
                    b, s = k - 2, q % 2
                    act.wait_ge(s_xht, b + 1)
                    wait(act, s_lg, b - 1)
                    cp(xhT[:, s].rearrange("p t c -> p (t c)"), bank[6][:, 0:T], bias=one_col[:]).then_inc(s_xhts, 1)
                if has[0]:
                    b, s = k, q % 2
                    act.wait_ge(s_z, b + 1)
                    wait(act, s_sc, b - 1)
                    cp(zT[:, s, :], bank[0][:, 0:T], bias=u_z[:]).then_inc(s_zs, 1)
                if has[1]:
                    b, s = k - 1, (q - 1) % 2
                    act.wait_ge(s_pt, b + 1)
                    wait(act, s_y, b - 1)
                    cp(prT[:, s].rearrange("p t c -> p (t c)"), bank[4][:, 0:3 * P]).then_inc(s_pts, 1)
                if has[0]:
                    b, s = k, q % 2
                    act.wait_ge(s_mx, b + 1)
                    wait(act, s_pt, b - 1)
                    wait(act, s_vv, b - 1)
                    act.activation(pr[:, s, 0, :], bank[2 + s][:, 0:P], ACT.Exp, bias=nmax[:, s, 0:1],
                                   accum_out=rsum[:, s, 0:1])
                    act.activation(pr[:, s, 1:3, :].rearrange("p t c -> p (t c)"), bank[2 + s][:, P:3 * P], ACT.Exp,
                                   bias=nmax[:, s, 1:2], accum_out=rsum[:, s, 1:2]).then_inc(s_p, 1)
                if has[1]:
                    b, s = k - 1, (q - 1) % 2
                    act.wait_ge(s_vv, b + 1)
                    act.activation(lnv[:, s], vv[:, s], ACT.Ln).then_inc(s_ln, 1)
                    act.wait_ge(s_ln, b + 1)
                    wait(act, s_xh, b - 1)
                    act.activation(rr[:, s], lnv[:, s], ACT.Exp, scale=-0.5).then_inc(s_rr, 1)
            run_steps(act, attend_step, NB + 2, U, 4, 2)
            act.wait_ge(s_gd, 1)
            act.activation(gates[:, :, 1], gd[:], ACT.Exp).then_inc(s_ge, 1)

            def ffn_step(k, q, use, known):
                if known is None or known < NTILE:
                    act.wait_ge(s_gt, k + 1)
                    wait(act, s_h, k - 1)
                    cp(xgT[:, q % 2, :], bank[q % 2][:, 0:P], bias=one_col[:]).then_inc(s_gts, 1)
                if known is None or 0 <= known - 1 < NTILE:
                    j, s = k - 1, (q - 1) % 2
                    act.wait_ge(s_h, j + 1)
                    wait(act, s_yy, j - 1)
                    act.activation(hs[:, s].rearrange("p h t -> p (h t)"), bank[2 + s][:], ACT.Gelu).then_inc(s_hs, 1)
            run_steps(act, ffn_step, NTILE + 1, 2, 4, 1)

        @block.vector
        def _(v):
            pg = Progress(v, s_dve)

            def op(ins):
                pg.did(ins)

            def rsqrt(out_, in_, t_i, t_f):
                op(v.tensor_scalar(t_i, in_.bitcast(I32), 1, None, ALU.logical_shift_right))
                pg.settle()
                op(v.tensor_scalar(out_.bitcast(I32), t_i, -1.0, RSQRT_GUESS, ALU.mult, ALU.add))
                pg.settle()
                for _ in range(3):
                    op(v.tensor_tensor(t_f, out_, out_, ALU.mult))
                    pg.settle()
                    op(v.tensor_tensor(t_f, t_f, in_, ALU.mult))
                    pg.settle()
                    op(v.tensor_scalar(t_f, t_f, -0.5, 1.5, ALU.mult, ALU.add))
                    pg.settle()
                    op(v.tensor_tensor(out_, out_, t_f, ALU.mult))
                    pg.settle()

            v.wait_ge(s_const, 1)
            with v.Fori(0, NCH // 2) as i:
                v.wait_ge(s_t1, i * 2 + 2)
                v.tensor_copy(xT[:, bass.ds(i * (2 * CH * P) + CH * P, CH * P)], bank[1][:]).then_inc(s_ev[1], 1)

            v.wait_ge(s_fold_pe, 1)
            v.wait_ge(s_par, 16 * N_PARAM)
            op(v.tensor_copy(aAT[:], bank[0][0:R, 0:P]))
            op(v.tensor_copy(pAT[:], bank[0][0:R, P:2 * P]))
            op(v.tensor_scalar(cov[:], bank[7][:, 0:P + 1], 1.0 / NTOK, None, ALU.mult))
            pg.settle()
            v.sem_inc(s_fold_dve, 1)
            v.wait_ge(s_fold_pe, 2)
            op(v.tensor_tensor(wm[:].rearrange("p a c -> p (a c)"), bank[1][:, 0:3 * P],
                               wa[:].rearrange("p a c -> p (a c)"), ALU.add))
            op(v.tensor_copy(wpmT[:], bank[2][:, 0:P]))
            op(v.tensor_copy(mu_row[:], bank[3][0:1, 0:P]))
            op(v.tensor_scalar(nmu_row[:], bank[3][0:1, 0:P], -1.0, None, ALU.mult))
            pg.settle()
            v.sem_inc(s_fold_dve, 1)
            v.wait_ge(s_fold_pe, 3)
            op(v.tensor_copy(wmT[:].rearrange("c (i a) -> c a i", a=3),
                             bank[0][:, 0:3 * P].rearrange("c (a i) -> c a i", a=3)))
            op(v.tensor_tensor(cov[:, 0:P], bank[3][:, P:2 * P], cov[:, 0:P], ALU.add))
            op(v.tensor_copy(wp2T[:], bank[2][:, P:2 * P]))
            pg.settle()
            v.sem_inc(s_fold_dve, 1)
            v.wait_ge(s_fold_pe, 4)
            pj = bank[1][:, 0:3 * (P + 1)].rearrange("p (g c) -> p g c", g=3)
            op(v.tensor_copy(wn[:].rearrange("p a c -> p (a c)"), bank[0][:, 0:3 * P]))
            op(v.tensor_copy(proj[:], pj))
            op(v.tensor_tensor(rl_d[:], rlb[:], rls[:], ALU.subtract))
            op(v.tensor_tensor(el_d[:], elb[:], els[:], ALU.subtract))
            pg.settle()
            for g in range(3):
                op(v.tensor_tensor(scr3[:, g, :], proj[:, g, 0:P], wn[:, g, :], ALU.mult))
            op(v.tensor_scalar(rl_bc[:], ones[:], rl_d[:], 1.0 / C, ALU.mult, ALU.mult))
            op(v.tensor_scalar(el_d[:], el_d[:], 1.0 / C, None, ALU.mult))
            pg.settle()
            op(v.tensor_reduce(bn[:, 0, :], scr3[:], AXX, ALU.add))
            pg.settle()
            op(v.tensor_scalar(bn[:, 0, :], bn[:, 0, :], EPS_BN, None, ALU.add))
            pg.settle()
            rsqrt(bn[:, 1, :], bn[:, 0, :], bn_i[:], bn[:, 3, :])
            op(v.tensor_tensor(bn[:, 1, :], bn[:, 1, :], gb[:, 0, :], ALU.mult))
            pg.settle()
            op(v.tensor_tensor(bn[:, 3, :], proj[:, :, P], bn[:, 1, :], ALU.mult))
            pg.settle()
            op(v.tensor_tensor(bn[:, 2, :], gb[:, 1, :], bn[:, 3, :], ALU.subtract))
            pg.settle()
            op(v.tensor_scalar(bn[:, 1:3, 0:1], bn[:, 1:3, 0:1], float(C) ** -0.5, None, ALU.mult))
            pg.settle()
            for g in range(3):
                op(v.tensor_scalar(wn[:, g, :], wn[:, g, :], bn[:, 1, g:g + 1], None, ALU.mult))
            op(v.tensor_scalar(tv_bc[:], ones[:], bn[:, 2, 2:3], None, ALU.mult))
            pg.settle()
            v.sem_inc(s_fold_dve, 1)
            v.wait_ge(s_fold_pe, 5)
            op(v.tensor_copy(MT[:], bank[2][:, 0:P]))
            op(v.tensor_copy(u_z[:], bank[2][:, P:P + 1]))
            op(v.tensor_copy(wvvT[:], bank[3][:, 0:P]))
            op(v.tensor_copy(cv[:], bank[3][:, P:2 * P]))
            op(v.scalar_tensor_tensor(out=RW[:], in0=rwT[:], scalar=rls[:], in1=bank[3][:, 2 * P:2 * P + E],
                                      op0=ALU.mult, op1=ALU.add))
            op(v.tensor_scalar(run[:, 0, 0, :], ebase[:], 1.0 / P, None, ALU.mult))
            pg.settle()
            v.sem_inc(s_fold_dve, 1)

            def expert_step(e, q, use, known):
                wait(v, s_w1f, e - 1)
                v.tensor_scalar(l_bc[:, q, :], ones[:], el_d[:, bass.ds(e, 1)], None, ALU.mult).then_inc(s_lbc, 1)
                v.wait_ge(s_w1f, e + 1)
                v.scalar_tensor_tensor(out=w1T[:, bass.ds(e, 1), :].rearrange("p a h -> p (a h)"),
                                       in0=w1raw[:, q, :], scalar=els[:, bass.ds(e, 1)], in1=bank[4 + q][:],
                                       op0=ALU.mult, op1=ALU.add).then_inc(s_w1o, 1)
            run_steps(v, expert_step, E, 2, 2, 0)

            cv_b = cv[:].unsqueeze(1).to_broadcast([P, TPB, P])
            lgb = bank[7][:, 0:TPB * E].rearrange("p (t e) -> p t e", e=E)
            rkb = bank[7][:, TPB * E:2 * TPB * E].rearrange("p (t e) -> p t e", e=E)

            def attend_step(k, q, use, known):
                has = [known is None or 0 <= known - d < NB for d in range(3)]
                if has[2]:
                    b, s = k - 2, q % 2
                    oh = oh_all[:, bass.ds(b * TPB, TPB), :, :]
                    v.wait_ge(s_lg, b + 1)
                    own_wait(v, s_own_dve)
                    for t in range(TPB):
                        op(v.max(mx8[:, t, :], lgb[:, t, :]))
                    pg.settle()
                    own_wait(v, s_own_dve)
                    for t in range(TPB):
                        op(v.max_index(ix8[:, t, :], mx8[:, t, :], lgb[:, t, :]))
                    op(v.tensor_copy(lg_all[:, bass.ds(b * TPB, TPB), :], mx8[:, :, 0:2]))
                    pg.settle()
                    op(v.tensor_tensor(ohc[:], iota_e[:].unsqueeze(1).to_broadcast([P, TPB * 2, E]),
                                       ix8[:, :, 0:2].unsqueeze(3).to_broadcast([P, TPB, 2, E]), ALU.is_equal))
                    pg.settle()
                    op(v.tensor_tensor(m_sum[:, s], ohc[:, :, 0, :], ohc[:, :, 1, :], ALU.add))
                    op(v.tensor_copy(oh, ohc[:]))
                    pg.settle()
                    op(v.tensor_tensor(run[:, s, 1, :], run[:, s, 0, :], m_sum[:, s, 0, :], ALU.add))
                    pg.settle()
                    wait(v, s_rk, b)
                    v.tensor_tensor(run[:, 1 - s, 0, :], run[:, s, 1, :], m_sum[:, s, 1, :],
                                    ALU.add).then_inc(s_oh, 1)
                if has[0]:
                    b, s = k, q % 2
                    v.wait_ge(s_v, b + 1)
                    wait(v, s_y, b - 1)
                    v.tensor_tensor(vs[:, s], bank[1][:, 0:T].rearrange("p (t c) -> p t c", c=P), cv_b,
                                    ALU.add).then_inc(s_vs, 1)
                    v.wait_ge(s_sc, b + 1)
                    wait(v, s_p, b - 1)
                    v.tensor_reduce(nmax[:, s, 0:1], bank[2 + s][:, 0:P], AXX, ALU.max, negate=True)
                    v.tensor_reduce(nmax[:, s, 1:2], bank[2 + s][:, P:3 * P], AXX, ALU.max,
                                    negate=True).then_inc(s_mx, 1)
                if has[1]:
                    b, s, slot = k - 1, (q - 1) % 2, (q - 1) % U
                    v.wait_ge(s_y, b + 1)
                    op(v.reciprocal(rinv[:], rsum[:, s, :]))
                    pg.settle()
                    for t in range(TPB):
                        op(v.scalar_tensor_tensor(
                            out=x1[:, t, :], in0=bank[5][:, t * P:(t + 1) * P], scalar=rinv[:, t:t + 1],
                            in1=x_all[:, bass.ds(b * TPB + t, 1), :].rearrange("p a c -> p (a c)"),
                            op0=ALU.mult, op1=ALU.add))
                    pg.settle()
                    for t in range(TPB):
                        op(v.bn_stats(st6[:, t, :], x1[:, t, :]))
                    pg.settle()
                    own_wait(v, s_own_dve)
                    for t in range(TPB):
                        op(v.bn_aggr(mv[:, t, :], st6[:, t, :]))
                    pg.settle()
                    op(v.tensor_scalar(vv[:, s, 0, :], mv[:, :, 1], EPS_POST, None, ALU.add))
                    v.tensor_scalar(vv[:, s, 1, :], mv[:, :, 1], 1.0 + EPS_FFN, EPS_POST * EPS_FFN, ALU.mult,
                                    ALU.add).then_inc(s_vv, 1)
                if has[2]:
                    b = k - 2
                    v.wait_ge(s_rk, b + 1)
                    op(v.tensor_tensor(ohr[:], ohc[:], rkb.unsqueeze(2).to_broadcast([P, TPB, 2, E]), ALU.mult))
                    pg.settle()
                    op(v.tensor_reduce(posf[:], ohr[:], AXX, ALU.add))
                    pg.settle()
                    op(v.tensor_copy(pos_all[:, bass.ds(b * TPB, TPB), :], posf[:]))
                    v.tensor_copy(pos_i[:, (q - 2) % U], posf[:]).then_inc(s_pos, 1)
                if has[1]:
                    b, s, slot = k - 1, (q - 1) % 2, (q - 1) % U
                    v.wait_ge(s_rr, b + 1)
                    for t in range(TPB):
                        op(v.tensor_scalar(x_all[:, bass.ds(b * TPB + t, 1), :].rearrange("p a c -> p (a c)"),
                                           x1[:, t, :], mv[:, t, 0:1], rr[:, s, 0, t:t + 1], ALU.subtract, ALU.mult))
                    wait(v, s_scat[slot], scat_need(use, q))
                    for t in range(TPB):
                        last = v.tensor_scalar(xh[:, slot, t, :], x1[:, t, :], mv[:, t, 0:1], rr[:, s, 1, t:t + 1],
                                               ALU.subtract, ALU.mult)
                    last.then_inc(s_xh, 1)

            def scat_need(use, q):
                r = use - 1 if q == 0 else use
                return r * (16 * 2 * TPB)
            PER_STEP = 9 + 8 + 3 + 2
            run_steps(v, attend_step, NB + 2, U, 5, 2, progress=pg, per_step=PER_STEP)

            op(v.tensor_tensor(gd[:], lg_all[:, :, 1], lg_all[:, :, 0], ALU.subtract))
            pg.settle()
            v.sem_inc(s_gd, 1)
            v.wait_ge(s_tot, 1)
            ends = bank[0][:, 0:E]
            op(v.tensor_scalar(padf[:], ends, part[:], None, ALU.add))
            op(v.tensor_tensor(cnt[:], ends, ebase[:], ALU.subtract))
            pg.settle()
            op(v.tensor_copy(padp[:], padf[:]))
            op(v.tensor_tensor(full[:], cnt[:].unsqueeze(2).to_broadcast([P, E, NT]),
                               kP_iota[:].unsqueeze(1).to_broadcast([P, E, NT]), ALU.is_gt))
            pg.settle()
            v.sem_inc(s_pad, 1)
            op(v.tensor_reduce(tiles[:], full[:], AXX, ALU.add))
            pg.settle()
            op(v.tensor_tensor_scan(out=incl[:], data0=ones[:, 0:E], data1=tiles[:], initial=0.0,
                                    op0=ALU.mult, op1=ALU.add))
            pg.settle()
            op(v.tensor_tensor(tb0[:], incl[:], tiles[:], ALU.subtract))
            op(v.tensor_scalar(shift[:, E:E + 1], incl[:, E - 1:E], -float(P), float(DUMMY), ALU.mult, ALU.add))
            pg.settle()
            op(v.scalar_tensor_tensor(out=shift[:, 0:E], in0=tb0[:], scalar=-float(P), in1=ebase[:],
                                      op0=ALU.mult, op1=ALU.add))
            op(v.tensor_tensor(cmp[:], j_iota[:].unsqueeze(2).to_broadcast([1, NTILE, E]),
                               incl[0:1, :].unsqueeze(1).to_broadcast([1, NTILE, E]), ALU.is_ge))
            pg.settle()
            op(v.tensor_reduce(ej[:], cmp[:], AXX, ALU.add))
            pg.settle()
            op(v.tensor_tensor(cmp9[:], ej[:].unsqueeze(2).to_broadcast([1, NTILE, E + 1]),
                               e_iota[:].unsqueeze(1).to_broadcast([1, NTILE, E + 1]), ALU.is_equal))
            op(v.tensor_scalar(tab_e[:], ej[:], float(E - 1), None, ALU.min))
            pg.settle()
            op(v.tensor_tensor(cmp9[:], cmp9[:], shift[0:1, :].unsqueeze(1).to_broadcast([1, NTILE, E + 1]), ALU.mult))
            pg.settle()
            op(v.tensor_reduce(rowf[:], cmp9[:], AXX, ALU.add))
            pg.settle()
            op(v.scalar_tensor_tensor(out=tab_row[:], in0=j_iota[:], scalar=float(P), in1=rowf[:],
                                      op0=ALU.mult, op1=ALU.add))
            pg.settle()
            v.sem_inc(s_tab, 1)

            def late_routing():
                op(v.tensor_tensor(ohs[:], oh_all[:].rearrange("p t k e -> p (t k) e"),
                                   shift[:, 0:E].unsqueeze(1).to_broadcast([P, NT * 2, E]), ALU.mult))
                v.wait_ge(s_ge, 1)
                op(v.tensor_scalar(gd[:], gates[:, :, 1], 1.0, None, ALU.add))
                pg.settle()
                op(v.tensor_reduce(yf[:], ohs[:], AXX, ALU.add))
                op(v.reciprocal(gates[:, :, 0], gd[:]))
                pg.settle()
                op(v.tensor_tensor(ypos[:].rearrange("p t k -> p (t k)"), pos_all[:].rearrange("p t k -> p (t k)"),
                                   yf[:], ALU.subtract))
                op(v.tensor_tensor(gates[:, :, 1], gates[:, :, 1], gates[:, :, 0], ALU.mult))
                pg.settle()
                v.sem_inc(s_gates, 1)
            late_routing()

            v.wait_ge(s_go, 16)

            def ffn_step(k, q, use, known):
                if known is None or known < NTILE:
                    e = v.value_load(tab_e[0:1, bass.ds(k, 1)], min_val=0, max_val=E - 1)
                    wait(v, s_h, k - 1)
                    v.tensor_copy(w1c[:, q % 2, :], w1T[:, bass.ds(e, 1), :].rearrange("p a h -> p (a h)")
                                  ).then_inc(s_w1s, 1)
                if known is None or 0 <= known - 2 < NTILE:
                    j, s, slot = k - 2, q % 2, (q - 2) % XR
                    e = v.value_load(tab_e[0:1, bass.ds(j, 1)], min_val=0, max_val=E - 1)
                    v.wait_ge(s_yy, j + 1)
                    wait(v, s_yo[slot], (use if q >= 2 else use - 1) * 16)
                    v.tensor_tensor(ysb[:, slot, :], bank[4 + s][:, 0:P],
                                    b2_bc[:, bass.ds(e, 1), :].rearrange("p a c -> p (a c)"), ALU.add
                                    ).then_inc(s_ys, 1)
            run_steps(v, ffn_step, NTILE + 2, XR, 6, 2)

            def comb_step(b, q, use, known):
                s = q % 2
                v.wait_ge(s_gy[s], (use * 2 + q // 2) * 64 + 64)
                for c in range(2):
                    for t in range(TPB):
                        base = x_all[:, bass.ds(b * TPB + t, 1), :].rearrange("p a c -> p (a c)") if c == 0 \
                            else acc[:, s, t, :]
                        op(v.scalar_tensor_tensor(
                            out=acc[:, s, t, :], in0=gy[:, s, t, c, :],
                            scalar=gates[:, bass.ds(b * TPB + t, 1), c], in1=base, op0=ALU.mult, op1=ALU.add))
                    pg.settle()
                v.sem_inc(s_comb, 1)
                for t in range(TPB):
                    op(v.bn_stats(st7[:, t, :], acc[:, s, t, :]))
                pg.settle()
                own_wait(v, s_own_dve)
                for t in range(TPB):
                    op(v.bn_aggr(mv7[:, t, :], st7[:, t, :]))
                pg.settle()
                op(v.tensor_scalar(v7[:], mv7[:, :, 1], EPS_POST, None, ALU.add))
                pg.settle()
                rsqrt(r7[:], v7[:], t7i[:], t7[:])
                wait(v, s_out[q], use * 16)
                v.tensor_scalar(osb[:, q, 0, :], acc[:, s, 0, :], mv7[:, 0, 0:1], r7[:, 0:1], ALU.subtract, ALU.mult)
                v.tensor_scalar(osb[:, q, 1, :], acc[:, s, 1, :], mv7[:, 1, 0:1], r7[:, 1:2], ALU.subtract,
                                ALU.mult).then_inc(s_os, 1)
            run_steps(v, comb_step, NB, 4, 4, 0, progress=pg, per_step=9 + RSQRT_OPS)


NAMES = ("x", "W_attn", "W_proj", "lora_attn_A", "lora_attn_B", "lora_proj_A", "lora_proj_B", "bn_gamma", "bn_beta")
FFN_NAMES = ("router_ln_scale", "router_ln_bias", "router_w", "router_b", "expert_ln_scale", "expert_ln_bias",
             "w1", "b1", "w2", "b2")


def kernel(**inputs):
    import numpy as np
    import concourse.bacc as bacc
    from concourse.bass_utils import run_bass_kernel_spmd

    nc = bacc.Bacc("TRN2", target_bir_lowering=False, num_devices=1)
    arrays, args = {}, []
    for name in ["L0_attn_" + n for n in NAMES] + ["L0_ffn_" + n for n in FFN_NAMES]:
        a = np.ascontiguousarray(inputs[name])
        arrays[name] = a
        args.append(nc.dram_tensor(name, a.shape, mybir.dt.from_np(a.dtype), kind="ExternalInput").ap())
    shape = inputs["L0_attn_x"].shape
    out = nc.dram_tensor("out", shape, F32, kind="ExternalOutput").ap()
    build(nc, *args, out)
    r = run_bass_kernel_spmd(nc, [arrays], core_ids=[0])
    return r.results[0]["out"]
```

```python
from contextlib import ExitStack

import concourse.bass as bass
from concourse import mybir

F32 = mybir.dt.float32
BF16 = mybir.dt.bfloat16
F16 = mybir.dt.float16
I32 = mybir.dt.int32
U32 = mybir.dt.uint32
ALU = mybir.AluOpType
ACT = mybir.ActivationFunctionType
AXX = mybir.AxisListType.X

P = 128
MASKED = -1e30
EPS_BN = 1e-5
EPS_POST = 1e-5
EPS_FFN = 1e-6
RSQRT_GUESS = float(0x5F3759DF)
RSQRT_OPS = 14


class Progress:

    def __init__(self, eng, sem):
        self.eng, self.sem, self.base, self.n = eng, sem, 0, 0

    def did(self, ins):
        ins.then_inc(self.sem, 1)
        self.n += 1

    def settle(self):
        self.eng.wait_ge(self.sem, self.base + self.n)


def wait(eng, sem, value):
    if isinstance(value, int) and value <= 0:
        return
    eng.wait_ge(sem, value)


def run_steps(eng, step, total, unroll, front, back, progress=None, per_step=0):
    loops = (total - front - back) // unroll
    for k in range(front):
        step(k, k % unroll, k // unroll, k)
    if loops:
        start = progress.n if progress else 0
        with eng.Fori(0, loops) as i:
            if progress:
                progress.base = eng.snap(i * (unroll * per_step))
            for j in range(front, front + unroll):
                step(eng.snap(i * unroll + j), j % unroll, eng.snap(i + j // unroll), None)
            if progress:
                assert progress.n - start == unroll * per_step, (progress.n - start, unroll * per_step)
        if progress:
            progress.base, progress.n = 0, start + loops * unroll * per_step
    for k in range(front + loops * unroll, total):
        step(k, k % unroll, k // unroll, k)


def build(nc, x, w_attn, w_proj, la_a, la_b, lp_a, lp_b, gamma, beta, r_ls, r_lb, r_w, r_b,
          e_ls, e_lb, w1, b1, w2, b2, out):
    NB, T, C = x.shape
    E, H, _ = w1.shape
    R = la_a.shape[1]
    HC = H // P
    NTOK = NB * T
    NT = NTOK // P
    TPB = T // P
    CAP = NTOK + P
    DUMMY = E * CAP
    NTILE = 2 * NT + E - 1 + 1
    NTILE += NTILE % 2
    assert C == P and TPB == 2

    queue = nc.dram_tensor("queue", [DUMMY + E * P, P], F32, kind="Internal").ap()
    yrows = nc.dram_tensor("yrows", [NTILE * P, P], F32, kind="Internal").ap()

    with ExitStack() as ctx:
        def sb(name, shape, dt=F32):
            return ctx.enter_context(nc.sbuf_tensor(name, shape, dt))

        def sem(name):
            return ctx.enter_context(nc.semaphore(name))

        bank = [ctx.enter_context(nc.psum_tensor(f"bank{i}", [P, 512], F32)) for i in range(8)]

        xT = sb("xT", [P, NTOK])
        x_all = sb("x_all", [P, NT, P])
        w1T = sb("w1T", [P, E, H])
        w2T = sb("w2T", [P, E, HC, P])
        b2_bc = sb("b2_bc", [P, E, P])
        oh_all = sb("oh_all", [P, NT, 2, E])
        pos_all = sb("pos_all", [P, NT, 2], I32)
        gates = sb("gates", [P, NT, 2])
        ypos = sb("ypos", [P, NT, 2], I32)

        late_used = [0]

        def late(shape):
            n, at = 1, late_used[0]
            for d in shape[1:]:
                n *= d
            late_used[0] += n
            assert late_used[0] <= NTOK
            names = "abcd"[:len(shape) - 1]
            return xT[:, at:at + n].rearrange(f"p ({' '.join(names)}) -> p {' '.join(names)}",
                                              **dict(zip(names, shape[1:])))

        ident = sb("ident", [P, P])
        ident_b = sb("ident_b", [P, P], BF16)
        mask_b = sb("mask_b", [P, P], BF16)
        before = sb("before", [P, P], F16)
        not_before = sb("not_before", [P, P], F16)
        ones_h = sb("ones_h", [P, P], F16)
        ones = sb("ones", [P, P])
        ones_b = sb("ones_b", [P, P], BF16)
        zeros = sb("zeros", [P, P])
        inv_c = sb("inv_c", [1, P])
        iota_e = sb("iota_e", [P, E])
        part = sb("part", [P, 1])
        one_col = sb("one_col", [P, 1])

        s_const, s_par, s_go = sem("s_const"), sem("s_par"), sem("s_go")
        s_pe, s_dve, s_act, s_pool = sem("s_pe"), sem("s_dve"), sem("s_act"), sem("s_pool")

        CH, RING = 4, 4
        NCH = NT // CH
        xin = sb("xin", [P, RING, CH, 132])
        s_xin = [sem(f"s_xin{i}") for i in range(RING)]
        s_t1, s_cp1 = sem("s_t1"), sem("s_cp1")
        s_ev = [sem("s_ev_act"), sem("s_ev_dve")]
        x_chunks = x.rearrange("b t c -> (b t) c").rearrange("(n j p) c -> n p j c", j=CH, p=P)

        wa = sb("wa", [P, 3, P])
        wp = sb("wp", [P, P])
        aA, aB = sb("aA", [P, R]), sb("aB", [R, 3 * P])
        pA, pB = sb("pA", [P, R]), sb("pB", [R, P])
        gb = sb("gb", [P, 2, 3])
        rls, rlb = sb("rls", [P, 1]), sb("rlb", [P, 1])
        els, elb = sb("els", [P, E]), sb("elb", [P, E])
        rwT, rb = sb("rwT", [P, E]), sb("rb", [1, E])
        aAT, pAT = sb("aAT", [R, P]), sb("pAT", [R, P])
        wm = sb("wm", [P, 3, P])
        wmT = sb("wmT", [P, 3 * P])
        wn = sb("wn", [P, 3, P])
        cov = sb("cov", [P, P + 1])
        mu_row, nmu_row = sb("mu_row", [1, P]), sb("nmu_row", [1, P])
        proj = sb("proj", [P, 3, P + 1])
        scr3 = sb("scr3", [P, 3, P])
        bn = sb("bn", [P, 4, 3])
        bn_i = sb("bn_i", [P, 3], I32)
        wpmT = sb("wpmT", [P, P])
        wp2T = sb("wp2T", [P, P])
        tv_bc = sb("tv_bc", [P, P])
        MT = sb("MT", [P, P])
        u_z = sb("u_z", [P, 1])
        wvvT = sb("wvvT", [P, P])
        cv = sb("cv", [P, P])
        cv3 = sb("cv3", [P, P], BF16)
        cvp = sb("cvp", [P, 3, P], BF16)
        rl_bc = sb("rl_bc", [P, P])
        rl_d = sb("rl_d", [P, 1])
        RW = sb("RW", [P, E])

        w1n = sb("w1n", [P, 2, HC, P])
        w2n = sb("w2n", [P, 2, H])
        b1r = sb("b1r", [1, 2, H])
        w1raw = sb("w1raw", [P, 2, H])
        l_bc = sb("l_bc", [P, 2, P])
        el_d = sb("el_d", [P, E])
        s_w = [sem("s_w0"), sem("s_w1")]
        s_w1t, s_w2t, s_w1c, s_w2c, s_lbc, s_w1f, s_w1o = [sem(n) for n in (
            "s_w1t", "s_w2t", "s_w1c", "s_w2c", "s_lbc", "s_w1f", "s_w1o")]

        U = 4
        xTs = sb("xTs", [P, 2, T])
        zT = sb("zT", [P, 2, T])
        vs = sb("vs", [P, U, TPB, P])
        nmax, rsum = sb("nmax", [P, 2, TPB]), sb("rsum", [P, U, TPB])
        rinv = sb("rinv", [P, 2, TPB])
        pr = sb("pr", [P, 2, 3, P])
        prT = sb("prT", [P, 2, 3, P])
        st6, mv = sb("st6", [P, TPB, 6]), sb("mv", [P, 2, TPB, 2])
        vv = sb("vv", [P, 2, 2, TPB])
        lnv = sb("lnv", [P, 2, 2, TPB])
        rr_all = sb("rr_all", [P, NB, 2, TPB])
        xh = sb("xh", [P, U, TPB, P])
        xhT = sb("xhT", [P, 2, TPB, P])
        mx8 = sb("mx8", [P, TPB, 8])
        ix8 = sb("ix8", [P, TPB, 8], U32)
        m_sum = sb("m_sum", [P, 2, TPB, E], F16)
        base_h = sb("base_h", [P, TPB, E], F16)
        ohr = sb("ohr", [P, TPB, 2, E])
        pos_i = sb("pos_i", [P, U, TPB, 2], I32)
        (s_xts, s_z, s_v, s_zs, s_vs, s_sc, s_mx, s_p, s_pt, s_pts, s_y, s_xh, s_xht, s_xhts,
         s_lg, s_oh, s_rk, s_pos, s_vv, s_ln, s_rr, s_yr, s_lr) = [sem(n) for n in (
            "s_xts", "s_z", "s_v", "s_zs", "s_vs", "s_sc", "s_mx", "s_p", "s_pt", "s_pts", "s_y", "s_xh",
            "s_xht", "s_xhts", "s_lg", "s_oh", "s_rk", "s_pos", "s_vv", "s_ln", "s_rr", "s_yr", "s_lr")]
        s_scat = [sem(f"s_scat{i}") for i in range(U)]

        cnt = sb("cnt", [P, E])
        tiles, incl, tb0 = sb("tiles", [P, E]), sb("incl", [P, E]), sb("tb0", [P, E])
        ebase = sb("ebase", [P, E])
        shift = sb("shift", [P, E + 1])
        e_iota = sb("e_iota", [1, E + 1])
        j_iota = sb("j_iota", [1, NTILE])
        cmp = sb("cmp", [1, NTILE, E])
        kP_iota = sb("kP_iota", [P, NT])
        full = sb("full", [P, E, NT])
        ej = sb("ej", [1, NTILE])
        cmp9 = sb("cmp9", [1, NTILE, E + 1])
        rowf = sb("rowf", [1, NTILE])
        tab_row, tab_e = sb("tab_row", [1, NTILE], I32), sb("tab_e", [1, NTILE], I32)
        padp = sb("padp", [P, E], I32)
        padf = sb("padf", [P, E])
        ohs = late([P, NT * 2, E])
        yf = sb("yf", [P, NT * 2])
        gd = sb("gd", [P, NT])
        s_tot, s_tab, s_pad, s_padd, s_zero, s_gd, s_ge, s_gates = [sem(n) for n in (
            "s_tot", "s_tab", "s_pad", "s_padd", "s_zero", "s_gd", "s_ge", "s_gates")]

        XR = 4
        xg = late([P, XR, P])
        xgT = late([P, 2, P])
        w1c = late([P, 2, H])
        hs = late([P, 2, HC, P])
        ysb = late([P, XR, P])
        s_xg = [sem(f"s_xg{i}") for i in range(XR)]
        s_yo = [sem(f"s_yo{i}") for i in range(XR)]
        s_gt, s_gts, s_w1s, s_h, s_hs, s_yy, s_ys = [sem(n) for n in (
            "s_gt", "s_gts", "s_w1s", "s_h", "s_hs", "s_yy", "s_ys")]

        gy = late([P, 2, TPB, 2, P])
        yidx = sb("yidx", [P, 2, TPB, 2], I32)
        acc = late([P, 2, TPB, P])
        osb = late([P, 4, TPB, P])
        st7, mv7, r7 = sb("st7", [P, TPB, 6]), sb("mv7", [P, TPB, 2]), sb("r7", [P, TPB])
        v7, t7, t7i = sb("v7", [P, TPB]), sb("t7", [P, TPB]), sb("t7i", [P, TPB], I32)
        s_yi, s_comb, s_os = sem("s_yi"), sem("s_comb"), sem("s_os")
        s_gy = [sem("s_gy0"), sem("s_gy1")]
        s_out = [sem(f"s_out{i}") for i in range(4)]

        N_PARAM = 14

        s_own_dve, s_own_pool = sem("s_own_dve"), sem("s_own_pool")

        def own_wait(eng, s_own):
            eng.sem_inc(s_own, 1)

        out_v = out.rearrange("b (j p) c -> b p j c", p=P)

        block = ctx.enter_context(nc.Block())

        @block.sync
        def _(sp):
            def load_chunk(c, slot):
                sp.dma_start(xin[:, slot, :, 0:P], x_chunks[c]).then_inc(s_xin[slot], 16)

            for c in range(RING):
                load_chunk(c, c)
            with nc.allow_non_contiguous_dma(reason="small parameters, transposed"):
                for dst, src in ((wa[:], w_attn.rearrange("(i a) c -> i a c", a=3)), (wp[:], w_proj),
                                 (aA[:], la_a), (aB[:], la_b), (pA[:], lp_a), (pB[:], lp_b),
                                 (gb[:, 0, :], gamma.rearrange("(a p) -> p a", p=P)),
                                 (gb[:, 1, :], beta.rearrange("(a p) -> p a", p=P)),
                                 (rls[:], r_ls.unsqueeze(1)), (rlb[:], r_lb.unsqueeze(1)),
                                 (rb[:], r_b.unsqueeze(0)), (rwT[:], r_w.rearrange("e d -> d e")),
                                 (els[:], e_ls.rearrange("e d -> d e")), (elb[:], e_lb.rearrange("e d -> d e"))):
                    sp.dma_start(dst, src).then_inc(s_par, 16)
            sp.dma_start(b2_bc[:], b2.partition_broadcast(P)).then_inc(s_go, 16)
            with sp.Fori(1, NCH // RING) as i:
                for j in range(RING):
                    sp.wait_ge(s_t1, i * RING + (j - RING + 1))
                    sp.wait_ge(s_cp1, i * RING + (j - RING + 1))
                    load_chunk(i * RING + j, j)
            wait(sp, s_const, 1)
            sp.dma_start(queue[DUMMY:DUMMY + E * P, :].rearrange("(a p) c -> p a c", p=P),
                         zeros[:, :].unsqueeze(1).to_broadcast([P, E, P])).then_inc(s_zero, 16)

            def load_expert(e, slot):
                wait(sp, s_w2t, e - 1)
                wait(sp, s_w1f, e - 1)
                sp.dma_start(w1n[:, slot], w1[e].rearrange("(k p) d -> p k d", p=P)).then_inc(s_w[slot], 16)
                sp.dma_start(w2n[:, slot], w2[e]).then_inc(s_w[slot], 16)
                sp.dma_start(b1r[:, slot], b1[e].unsqueeze(0)).then_inc(s_w[slot], 16)
            for e in range(2):
                load_expert(e, e)
            with sp.Fori(1, E // 2) as i:
                for j in range(2):
                    load_expert(sp.snap(i * 2 + j), j)

            for q in range(U):
                sp.wait_ge(s_scat[q], 16 * 2 * TPB * (NB // U))
            sp.wait_ge(s_padd, 16 * E)
            sp.wait_ge(s_zero, 16)
            sp.wait_ge(s_tab, 1)

            def load_rows(j, slot):
                wait(sp, s_gt, j - XR + 1)
                row = sp.value_load(tab_row[0:1, bass.ds(j, 1)], min_val=0, max_val=DUMMY + (E - 1) * P)
                sp.dma_start(xg[:, slot], queue[bass.ds(row, P), :]).then_inc(s_xg[slot], 16)

            def ffn_step(k, slot, use, known):
                if known is None or known < NTILE:
                    load_rows(k, slot)
                if known is None or known >= 4:
                    j = k - 4
                    wait(sp, s_ys, j + 1)
                    sp.dma_start(yrows[bass.ds(j * P, P), :], ysb[:, slot]).then_inc(s_yo[slot], 16)
            run_steps(sp, ffn_step, NTILE + 4, XR, 4, 4)

            def store_step(b, slot, use, known):
                wait(sp, s_os, b + 1)
                sp.dma_start(out_v[b], osb[:, slot]).then_inc(s_out[slot], 16)
            run_steps(sp, store_step, NB, 4, 0, 0)
            for q in range(4):
                sp.wait_ge(s_out[q], 16 * (NB // 4))

        @block.gpsimd
        def _(pool):
            pg = Progress(pool, s_pool)
            pg.did(pool.memset(ones[:], 1.0))
            pg.did(pool.memset(ones_b[:], 1.0))
            pg.did(pool.memset(ones_h[:], 1.0))
            pg.did(pool.memset(cv3[:], 0.0))
            pg.did(pool.iota(base_h[:], [[0, TPB], [CAP // P, E]], base=0, channel_multiplier=0,
                             allow_small_or_imprecise_dtypes=True))
            pg.did(pool.memset(zeros[:], 0.0))
            pg.did(pool.memset(inv_c[:], 1.0 / C))
            pg.did(pool.memset(one_col[:], 1.0))
            for s in range(RING):
                pg.did(pool.memset(xin[:, s, :, P:P + 1], 1.0))
            pg.did(pool.memset(mask_b[:], 0.0))
            pg.did(pool.iota(iota_e[:], [[1, E]], base=0, channel_multiplier=0, allow_small_or_imprecise_dtypes=True))
            pg.did(pool.iota(e_iota[:], [[1, E + 1]], base=0, channel_multiplier=0, allow_small_or_imprecise_dtypes=True))
            pg.did(pool.iota(j_iota[:], [[1, NTILE]], base=0, channel_multiplier=0, allow_small_or_imprecise_dtypes=True))
            pg.did(pool.iota(kP_iota[:], [[P, NT]], base=0, channel_multiplier=0, allow_small_or_imprecise_dtypes=True))
            pg.did(pool.iota(part[:], [[0, 1]], base=0, channel_multiplier=1, allow_small_or_imprecise_dtypes=True))
            pg.did(pool.iota(ebase[:], [[CAP, E]], base=0, channel_multiplier=0, allow_small_or_imprecise_dtypes=True))
            pg.settle()
            pg.did(pool.affine_select(out=ident[:], in_=ones[:], pattern=[[-1, P]], compare_op=ALU.is_equal,
                                      fill=0.0, base=0, channel_multiplier=1))
            pg.did(pool.affine_select(out=ident_b[:], in_=ones_b[:], pattern=[[-1, P]], compare_op=ALU.is_equal,
                                      fill=0.0, base=0, channel_multiplier=1))
            pg.did(pool.affine_select(out=mask_b[:], in_=mask_b[:], pattern=[[-1, P]], compare_op=ALU.is_ge,
                                      fill=MASKED, base=0, channel_multiplier=1))
            pg.did(pool.affine_select(out=before[:], in_=ones_h[:], pattern=[[1, P]], compare_op=ALU.is_gt,
                                      fill=0.0, base=0, channel_multiplier=-1))
            pg.did(pool.affine_select(out=not_before[:], in_=ones_h[:], pattern=[[-1, P]], compare_op=ALU.is_ge,
                                      fill=0.0, base=0, channel_multiplier=1))
            pg.settle()
            pool.sem_inc(s_const, 1)
            with pool.Fori(0, NCH // RING) as i:
                for j in range(RING):
                    pool.wait_ge(s_xin[j], i * 16 + 16)
                    pool.tensor_copy(x_all[:, bass.ds(i * (RING * CH) + j * CH, CH), :],
                                     xin[:, j, :, 0:P]).then_inc(s_cp1, 1)
            def scatter_step(b, q, use, known):
                wait(pool, s_pos, b + 1)
                own_wait(pool, s_own_pool)
                for t in range(TPB):
                    for c in range(2):
                        pool.indirect_dma_start(
                            out=queue, out_offset=bass.IndirectOffsetOnAxis(pos_i[:, q, t, c:c + 1], 0),
                            in_=xh[:, q, t, :], in_offset=None).then_inc(s_scat[q], 16)
            run_steps(pool, scatter_step, NB, U, 0, 0)
            pool.wait_ge(s_pad, 1)
            for e in range(E):
                pool.indirect_dma_start(out=queue, out_offset=bass.IndirectOffsetOnAxis(padp[:, e:e + 1], 0),
                                        in_=zeros[:], in_offset=None).then_inc(s_padd, 16)
            for q in range(XR):
                n = len(range(q, NTILE, XR))
                pool.wait_ge(s_yo[q], 16 * n)

            def gather_step(b, q, use, known):
                s = q % 2
                wait(pool, s_comb, b - 1)
                pool.tensor_copy(yidx[:, s], ypos[:, bass.ds(b * TPB, TPB), :]).then_inc(s_yi, 1)
                wait(pool, s_yi, b + 1)
                own_wait(pool, s_own_pool)
                for t in range(TPB):
                    for c in range(2):
                        pool.indirect_dma_start(
                            out=gy[:, s, t, c, :], out_offset=None, in_=yrows,
                            in_offset=bass.IndirectOffsetOnAxis(yidx[:, s, t, c:c + 1], 0)).then_inc(s_gy[s], 16)
            run_steps(pool, gather_step, NB, 2, 2, 0)

        s_fold_pe, s_fold_dve = sem("s_fold_pe"), sem("s_fold_dve")

        @block.tensor
        def _(pe):
            mm, tr = pe.matmul, pe.transpose
            pe.wait_ge(s_const, 1)
            gram = bank[7][:, 0:P + 1]

            def gram_zero(start):
                return mm(gram, zeros[:], xin[:, 0, 0, 0:P + 1], start=start, stop=not start)

            pe.wait_ge(s_xin[0], 16)
            gram_zero(True)

            def chunk_step(k, q, use, known):
                pe.wait_ge(s_xin[q], use * 16 + 16)
                wait(pe, s_ev[q % 2], use * 2 + q // 2)
                for t in range(CH):
                    tr(bank[q % 2][:, t * P:(t + 1) * P], xin[:, q, t, 0:P], ident[:])
                for t in range(CH):
                    last = mm(gram, xin[:, q, t, 0:P], xin[:, q, t, 0:P + 1], start=False, stop=False)
                last.then_inc(s_t1, 1)
            run_steps(pe, chunk_step, NCH, RING, RING, 0)
            gram_zero(False)

            def round_opens(r):
                wait(pe, s_fold_dve, r)

            pe.wait_ge(s_par, 16 * N_PARAM)
            for h in range(2):
                pe.wait_ge(s_ev[h], NCH // 2)
            tr(bank[0][0:R, 0:P], aA[:], ident[:])
            tr(bank[0][0:R, P:2 * P], pA[:], ident[:]).then_inc(s_fold_pe, 1)
            round_opens(1)
            mm(bank[1][:, 0:3 * P], aAT[:], aB[:], start=True, stop=True)
            mm(bank[2][:, 0:P], wp[:], ident[:], start=True, stop=False)
            mm(bank[2][:, 0:P], pB[:], pAT[:], start=False, stop=True)
            mm(bank[3][0:1, 0:P], cov[:, P:P + 1], ident[:], start=True, stop=True).then_inc(s_fold_pe, 1)
            round_opens(2)
            for a in range(3):
                tr(bank[0][:, a * P:(a + 1) * P], wm[:, a, :], ident[:])
            mm(bank[3][:, P:2 * P], nmu_row[:], mu_row[:], start=True, stop=True)
            mm(bank[2][:, P:2 * P], wp[:], wpmT[:], start=True, stop=True).then_inc(s_fold_pe, 1)
            round_opens(3)
            for g in range(3):
                tr(bank[0][:, g * P:(g + 1) * P], wmT[:, g * P:(g + 1) * P], ident[:])
            for g in range(3):
                last = mm(bank[1][:, g * (P + 1):(g + 1) * (P + 1)], wmT[:, g * P:(g + 1) * P], cov[:],
                          start=True, stop=True)
            last.then_inc(s_fold_pe, 1)
            round_opens(4)
            mm(bank[2][:, 0:P], wn[:, 0, :], wn[:, 1, :], start=True, stop=True)
            mm(bank[2][:, P:P + 1], wn[:, 1, :], bn[:, 2, 0:1], start=True, stop=True)
            mm(bank[3][:, 0:P], wn[:, 2, :], wp2T[:], start=True, stop=True)
            mm(bank[3][:, P:2 * P], tv_bc[:], wp2T[:], start=True, stop=True)
            mm(bank[3][:, 2 * P:2 * P + E], rl_bc[:], rwT[:], start=True, stop=False)
            mm(bank[3][:, 2 * P:2 * P + E], inv_c[:], rb[:], start=False, stop=True).then_inc(s_fold_pe, 1)
            round_opens(5)

            def expert_step(e, q, use, known):
                pe.wait_ge(s_w[q], use * 48 + 48)
                wait(pe, s_w1c, e - 1)
                wait(pe, s_w2c, e - 1)
                for h in range(HC):
                    last = tr(bank[q][:, h * P:(h + 1) * P], w1n[:, q, h, :], ident[:])
                last.then_inc(s_w1t, 1)
                for h in range(HC):
                    last = tr(bank[2 + q][:, h * P:(h + 1) * P], w2n[:, q, h * P:(h + 1) * P], ident[:])
                last.then_inc(s_w2t, 1)
                pe.wait_ge(s_w1c, e + 1)
                pe.wait_ge(s_lbc, e + 1)
                wait(pe, s_w1o, e - 1)
                mm(bank[4 + q][:], l_bc[:, q, :], w1raw[:, q, :], start=True, stop=False)
                mm(bank[4 + q][:], inv_c[:], b1r[:, q, :], start=False, stop=True).then_inc(s_w1f, 1)
            run_steps(pe, expert_step, E, 2, 2, 0)
            pe.wait_ge(s_w2c, E)
            pe.wait_ge(s_w1o, E)

            pe.wait_ge(s_fold_dve, 5)
            tally = bank[7][:, 0:TPB * E]
            logits = bank[5][:, T:T + TPB * E]

            def add(t, weights, m, **kw):
                return mm(bank[7][:, t * E:(t + 1) * E], weights[:], m, skip_group_check=True, **kw)

            mm(tally, ones_h[:], base_h[:].rearrange("p t e -> p (t e)"), start=True, stop=False,
               skip_group_check=True)

            def rank_rest(s):
                for t in range(TPB):
                    add(t, not_before, m_sum[:, s, t, :], start=False, stop=False)
                return add(0, ones_h, m_sum[:, s, 1, :], start=False, stop=False)

            def z_and_v(b, s, q):
                pe.wait_ge(s_xts, b + 1)
                wait(pe, s_zs, b)
                mm(bank[0][:, 0:T], MT[:], xTs[:, s, :], start=True, stop=True).then_inc(s_z, 1)
                wait(pe, s_vs, b)
                for t in range(TPB):
                    o = bank[1][:, t * P:(t + 1) * P]
                    mm(o, ones_b[:], cv3[:], start=True, stop=False)
                    last = mm(o, xTs[:, s, t * P:(t + 1) * P], wvvT[:], start=False, stop=True)
                last.then_inc(s_v, 1)

            def scores(b, s):
                pe.wait_ge(s_zs, b + 1)
                wait(pe, s_p, b - 1)
                sc = bank[2 + s]
                mm(sc[:, 0:P], ident_b[:], mask_b[:], start=True, stop=False)
                mm(sc[:, 0:P], zT[:, s, 0:P], xTs[:, s, 0:P], start=False, stop=True)
                mm(sc[:, P:2 * P], zT[:, s, P:T], xTs[:, s, 0:P], start=True, stop=True)
                mm(sc[:, 2 * P:3 * P], ident_b[:], mask_b[:], start=True, stop=False)
                mm(sc[:, 2 * P:3 * P], zT[:, s, P:T], xTs[:, s, P:T], start=False, stop=True).then_inc(s_sc, 1)

            def attend_step(k, q, use, known):
                has = {d: known is None or 0 <= known - d < NB for d in (-1, 1, 3, 4)}
                if known == 0:
                    z_and_v(0, 0, 0)
                    scores(0, 0)
                if has[1]:
                    b, s = k - 1, (q - 1) % 2
                    pe.wait_ge(s_p, b + 1)
                    wait(pe, s_pts, b)
                    for n in range(3):
                        last = tr(bank[4][:, n * P:(n + 1) * P], pr[:, s, n, :], ident[:])
                    last.then_inc(s_pt, 1)
                if has[-1]:
                    z_and_v(k + 1, (q + 1) % 2, q + 1)
                if has[3]:
                    b = k - 3
                    pe.wait_ge(s_xh, b + 1)
                    wait(pe, s_xhts, b)
                    for t in range(TPB):
                        last = tr(bank[6][:, t * P:(t + 1) * P], xh[:, (q - 3) % U, t, :], ident[:])
                    last.then_inc(s_xht, 1)
                if has[-1]:
                    scores(k + 1, (q + 1) % 2)
                if has[1]:
                    b, s = k - 1, (q - 1) % 2
                    pe.wait_ge(s_pts, b + 1)
                    pe.wait_ge(s_vs, b + 1)
                    wait(pe, s_yr, b)
                    wait(pe, s_lr, b - 2)
                    v0, v1 = vs[:, (q - 1) % U, 0, :], vs[:, (q - 1) % U, 1, :]
                    mm(bank[5][:, 0:P], prT[:, s, 0, :], v0, start=True, stop=True)
                    mm(bank[5][:, P:T], prT[:, s, 1, :], v0, start=True, stop=False)
                    mm(bank[5][:, P:T], prT[:, s, 2, :], v1, start=False, stop=True).then_inc(s_y, 1)
                if has[3]:
                    b, s = k - 3, (q - 3) % 2
                    pe.wait_ge(s_xhts, b + 1)
                    wait(pe, s_lr, b)
                    for t in range(TPB):
                        last = mm(logits[:, t * E:(t + 1) * E], xhT[:, s, t, :], RW[:],
                                  start=True, stop=True)
                    last.then_inc(s_lg, 1)
                if has[4]:
                    b, s = k - 4, q % 2
                    pe.wait_ge(s_oh, b + 1)
                    wait(pe, s_pos, b)
                    if known is None or known > 4:
                        rank_rest(1 - s)
                    add(0, before, m_sum[:, s, 0, :], start=False, stop=False)
                    add(1, ones_h, m_sum[:, s, 0, :], start=False, stop=False)
                    add(1, before, m_sum[:, s, 1, :], start=False, stop=False).then_inc(s_rk, 1)
            run_steps(pe, attend_step, NB + 4, U, 5, 4)
            pe.wait_ge(s_pos, NB)
            rank_rest((NB - 1) % 2).then_inc(s_tot, 1)

            pe.wait_ge(s_tab, 1)

            def ffn_step(k, q, use, known):
                if known is None or known < NTILE:
                    pe.wait_ge(s_xg[q], use * 16 + 16)
                    wait(pe, s_gts, k - 1)
                    tr(bank[q % 2][:, 0:P], xg[:, q, :], ident[:]).then_inc(s_gt, 1)
                if known is None or 0 <= known - 1 < NTILE:
                    j, s = k - 1, (q - 1) % 2
                    pe.wait_ge(s_gts, j + 1)
                    pe.wait_ge(s_w1s, j + 1)
                    wait(pe, s_hs, j - 1)
                    for h in range(HC):
                        last = mm(bank[2 + s][:, h * P:(h + 1) * P], w1c[:, s, h * P:(h + 1) * P], xgT[:, s, :],
                                  start=True, stop=True)
                    last.then_inc(s_h, 1)
                if known is None or 0 <= known - 2 < NTILE:
                    j, s = k - 2, q % 2
                    e = pe.value_load(tab_e[0:1, bass.ds(j, 1)], min_val=0, max_val=E - 1)
                    pe.wait_ge(s_hs, j + 1)
                    wait(pe, s_ys, j - 1)
                    for h in range(HC):
                        last = mm(bank[4 + s][:, 0:P], hs[:, s, h, :],
                                  w2T[:, bass.ds(e, 1), h, :].rearrange("p a d -> p (a d)"),
                                  start=(h == 0), stop=(h == HC - 1))
                    last.then_inc(s_yy, 1)
            run_steps(pe, ffn_step, NTILE + 2, XR, 4, 2)

        @block.scalar
        def _(act):
            def cp(out_, in_, bias=0.0):
                return act.activation(out_, in_, ACT.Identity, bias=bias)

            act.wait_ge(s_const, 1)
            with act.Fori(0, NCH // 2) as i:
                act.wait_ge(s_t1, i * 2 + 1)
                cp(xT[:, bass.ds(i * (2 * CH * P), CH * P)], bank[0][:]).then_inc(s_ev[0], 1)

            def expert_step(e, q, use, known):
                act.wait_ge(s_w1t, e + 1)
                wait(act, s_w1o, e - 1)
                cp(w1raw[:, q, :], bank[q][:]).then_inc(s_w1c, 1)
                act.wait_ge(s_w2t, e + 1)
                cp(w2T[:, bass.ds(e, 1), :, :].rearrange("p a h d -> p (a h d)"), bank[2 + q][:]).then_inc(s_w2c, 1)
            run_steps(act, expert_step, E, 2, 2, 0)

            act.preload_act_table_set("natural_log_exp_and_others")
            for h in range(2):
                act.wait_ge(s_ev[h], NCH // 2)
            act.wait_ge(s_fold_dve, 5)

            def copy_xT(b, s):
                wait(act, s_sc, b - 1)
                cp(xTs[:, s, :], xT[:, bass.ds(b * T, T)]).then_inc(s_xts, 1)

            def copy_z_v(b, q):
                act.wait_ge(s_z, b + 1)
                wait(act, s_sc, b - 1)
                cp(zT[:, q % 2, :], bank[0][:, 0:T], bias=u_z[:]).then_inc(s_zs, 1)
                act.wait_ge(s_v, b + 1)
                wait(act, s_y, b - U + 1)
                cp(vs[:, q % U].rearrange("p t c -> p (t c)"), bank[1][:, 0:T]).then_inc(s_vs, 1)

            def attend_step(k, q, use, known):
                has = {d: known is None or 0 <= known - d < NB for d in (-2, -1, 0, 1, 2, 3)}
                if known == 0:
                    copy_xT(0, 0)
                    copy_xT(1, 1)
                    copy_z_v(0, 0)
                if has[0]:
                    b, s = k, q % 2
                    act.wait_ge(s_mx, b + 1)
                    wait(act, s_pt, b - 1)
                    wait(act, s_yr, b - U + 1)
                    act.activation(pr[:, s, 0, :], bank[2 + s][:, 0:P], ACT.Exp, bias=nmax[:, s, 0:1],
                                   accum_out=rsum[:, q % U, 0:1])
                    act.activation(pr[:, s, 1:3, :].rearrange("p t c -> p (t c)"), bank[2 + s][:, P:3 * P], ACT.Exp,
                                   bias=nmax[:, s, 1:2], accum_out=rsum[:, q % U, 1:2]).then_inc(s_p, 1)
                if has[1]:
                    b, s = k - 1, (q - 1) % 2
                    act.wait_ge(s_pt, b + 1)
                    wait(act, s_y, b - 1)
                    cp(prT[:, s].rearrange("p t c -> p (t c)"), bank[4][:, 0:3 * P]).then_inc(s_pts, 1)
                if has[-1]:
                    copy_z_v(k + 1, q + 1)
                if has[3]:
                    b, s = k - 3, (q - 3) % 2
                    act.wait_ge(s_xht, b + 1)
                    wait(act, s_lg, b - 1)
                    cp(xhT[:, s].rearrange("p t c -> p (t c)"), bank[6][:, 0:T], bias=one_col[:]).then_inc(s_xhts, 1)
                if has[-2]:
                    copy_xT(k + 2, q % 2)
                if has[2]:
                    b, s = k - 2, q % 2
                    act.wait_ge(s_vv, b + 1)
                    act.activation(lnv[:, s], vv[:, s], ACT.Ln).then_inc(s_ln, 1)
                    act.wait_ge(s_ln, b + 1)
                    act.activation(rr_all[:, bass.ds(b, 1), :, :].rearrange("p a n t -> p (a n) t"), lnv[:, s], ACT.Exp,
                                   scale=-0.5).then_inc(s_rr, 1)
            run_steps(act, attend_step, NB + 3, U, 5, 3)
            act.wait_ge(s_gd, 1)
            act.activation(gates[:, :, 1], gd[:], ACT.Exp).then_inc(s_ge, 1)

            def ffn_step(k, q, use, known):
                if known is None or known < NTILE:
                    act.wait_ge(s_gt, k + 1)
                    wait(act, s_h, k - 1)
                    cp(xgT[:, q % 2, :], bank[q % 2][:, 0:P], bias=one_col[:]).then_inc(s_gts, 1)
                if known is None or 0 <= known - 1 < NTILE:
                    j, s = k - 1, (q - 1) % 2
                    act.wait_ge(s_h, j + 1)
                    wait(act, s_yy, j - 1)
                    act.activation(hs[:, s].rearrange("p h t -> p (h t)"), bank[2 + s][:], ACT.Gelu).then_inc(s_hs, 1)
            run_steps(act, ffn_step, NTILE + 1, 2, 4, 1)

        @block.vector
        def _(v):
            pg = Progress(v, s_dve)

            def op(ins):
                pg.did(ins)

            def rsqrt(out_, in_, t_i, t_f):
                op(v.tensor_scalar(t_i, in_.bitcast(I32), 1, None, ALU.logical_shift_right))
                pg.settle()
                op(v.tensor_scalar(out_.bitcast(I32), t_i, -1.0, RSQRT_GUESS, ALU.mult, ALU.add))
                pg.settle()
                for _ in range(3):
                    op(v.tensor_tensor(t_f, out_, out_, ALU.mult))
                    pg.settle()
                    op(v.tensor_tensor(t_f, t_f, in_, ALU.mult))
                    pg.settle()
                    op(v.tensor_scalar(t_f, t_f, -0.5, 1.5, ALU.mult, ALU.add))
                    pg.settle()
                    op(v.tensor_tensor(out_, out_, t_f, ALU.mult))
                    pg.settle()

            v.wait_ge(s_const, 1)
            with v.Fori(0, NCH // 2) as i:
                v.wait_ge(s_t1, i * 2 + 2)
                v.tensor_copy(xT[:, bass.ds(i * (2 * CH * P) + CH * P, CH * P)], bank[1][:]).then_inc(s_ev[1], 1)

            v.wait_ge(s_fold_pe, 1)
            v.wait_ge(s_par, 16 * N_PARAM)
            op(v.tensor_copy(aAT[:], bank[0][0:R, 0:P]))
            op(v.tensor_copy(pAT[:], bank[0][0:R, P:2 * P]))
            op(v.tensor_scalar(cov[:], bank[7][:, 0:P + 1], 1.0 / NTOK, None, ALU.mult))
            pg.settle()
            v.sem_inc(s_fold_dve, 1)
            v.wait_ge(s_fold_pe, 2)
            op(v.tensor_tensor(wm[:].rearrange("p a c -> p (a c)"), bank[1][:, 0:3 * P],
                               wa[:].rearrange("p a c -> p (a c)"), ALU.add))
            op(v.tensor_copy(wpmT[:], bank[2][:, 0:P]))
            op(v.tensor_copy(mu_row[:], bank[3][0:1, 0:P]))
            op(v.tensor_scalar(nmu_row[:], bank[3][0:1, 0:P], -1.0, None, ALU.mult))
            pg.settle()
            v.sem_inc(s_fold_dve, 1)
            v.wait_ge(s_fold_pe, 3)
            op(v.tensor_copy(wmT[:].rearrange("c (i a) -> c a i", a=3),
                             bank[0][:, 0:3 * P].rearrange("c (a i) -> c a i", a=3)))
            op(v.tensor_tensor(cov[:, 0:P], bank[3][:, P:2 * P], cov[:, 0:P], ALU.add))
            op(v.tensor_copy(wp2T[:], bank[2][:, P:2 * P]))
            pg.settle()
            v.sem_inc(s_fold_dve, 1)
            v.wait_ge(s_fold_pe, 4)
            pj = bank[1][:, 0:3 * (P + 1)].rearrange("p (g c) -> p g c", g=3)
            op(v.tensor_copy(wn[:].rearrange("p a c -> p (a c)"), bank[0][:, 0:3 * P]))
            op(v.tensor_copy(proj[:], pj))
            op(v.tensor_tensor(rl_d[:], rlb[:], rls[:], ALU.subtract))
            op(v.tensor_tensor(el_d[:], elb[:], els[:], ALU.subtract))
            pg.settle()
            for g in range(3):
                op(v.tensor_tensor(scr3[:, g, :], proj[:, g, 0:P], wn[:, g, :], ALU.mult))
            op(v.tensor_scalar(rl_bc[:], ones[:], rl_d[:], 1.0 / C, ALU.mult, ALU.mult))
            op(v.tensor_scalar(el_d[:], el_d[:], 1.0 / C, None, ALU.mult))
            pg.settle()
            op(v.tensor_reduce(bn[:, 0, :], scr3[:], AXX, ALU.add))
            pg.settle()
            op(v.tensor_scalar(bn[:, 0, :], bn[:, 0, :], EPS_BN, None, ALU.add))
            pg.settle()
            rsqrt(bn[:, 1, :], bn[:, 0, :], bn_i[:], bn[:, 3, :])
            op(v.tensor_tensor(bn[:, 1, :], bn[:, 1, :], gb[:, 0, :], ALU.mult))
            pg.settle()
            op(v.tensor_tensor(bn[:, 3, :], proj[:, :, P], bn[:, 1, :], ALU.mult))
            pg.settle()
            op(v.tensor_tensor(bn[:, 2, :], gb[:, 1, :], bn[:, 3, :], ALU.subtract))
            pg.settle()
            op(v.tensor_scalar(bn[:, 1:3, 0:1], bn[:, 1:3, 0:1], float(C) ** -0.5, None, ALU.mult))
            pg.settle()
            for g in range(3):
                op(v.tensor_scalar(wn[:, g, :], wn[:, g, :], bn[:, 1, g:g + 1], None, ALU.mult))
            op(v.tensor_scalar(tv_bc[:], ones[:], bn[:, 2, 2:3], None, ALU.mult))
            pg.settle()
            v.sem_inc(s_fold_dve, 1)
            v.wait_ge(s_fold_pe, 5)
            op(v.tensor_copy(MT[:], bank[2][:, 0:P]))
            op(v.tensor_copy(u_z[:], bank[2][:, P:P + 1]))
            op(v.tensor_copy(wvvT[:], bank[3][:, 0:P]))
            op(v.tensor_copy(cv[:], bank[3][:, P:2 * P]))
            op(v.scalar_tensor_tensor(out=RW[:], in0=rwT[:], scalar=rls[:], in1=bank[3][:, 2 * P:2 * P + E],
                                      op0=ALU.mult, op1=ALU.add))
            pg.settle()
            for n in range(3):
                op(v.tensor_copy(cvp[:, n, :], cv[:]))
                pg.settle()
                op(v.tensor_copy(cv3[32 * n:32 * n + 1, :], cvp[32 * n:32 * n + 1, n, :]))
                if n < 2:
                    op(v.tensor_tensor(cv[:], cv[:], cvp[:, n, :], ALU.subtract))
                pg.settle()
            v.sem_inc(s_fold_dve, 1)

            def expert_step(e, q, use, known):
                wait(v, s_w1f, e - 1)
                v.tensor_scalar(l_bc[:, q, :], ones[:], el_d[:, bass.ds(e, 1)], None, ALU.mult).then_inc(s_lbc, 1)
                v.wait_ge(s_w1f, e + 1)
                v.scalar_tensor_tensor(out=w1T[:, bass.ds(e, 1), :].rearrange("p a h -> p (a h)"),
                                       in0=w1raw[:, q, :], scalar=els[:, bass.ds(e, 1)], in1=bank[4 + q][:],
                                       op0=ALU.mult, op1=ALU.add).then_inc(s_w1o, 1)
            run_steps(v, expert_step, E, 2, 2, 0)

            v.wait_ge(s_cp1, NCH)
            lgb = bank[5][:, T:T + TPB * E].rearrange("p (t e) -> p t e", e=E)
            rkb = bank[7][:, 0:TPB * E].rearrange("p (t e) -> p t e", e=E)

            def x_row(b, t):
                return x_all[:, bass.ds(b * TPB + t, 1), :].rearrange("p a c -> p (a c)")

            def attend_step(k, q, use, known):
                has = {d: known is None or 0 <= known - d < NB for d in (0, 1, 2, 3, 4, 5)}
                b2, q2, s2 = k - 2, (q - 2) % U, q % 2
                b4, s4 = k - 4, q % 2
                b5, q5 = k - 5, (q - 5) % U

                def one_hots(b):
                    return oh_all[:, bass.ds(b * TPB, TPB), :, :]

                if has[0]:
                    b, s = k, q % 2
                    v.wait_ge(s_sc, b + 1)
                    wait(v, s_p, b - 1)
                    v.tensor_reduce(nmax[:, s, 0:1], bank[2 + s][:, 0:P], AXX, ALU.max, negate=True)
                    v.tensor_reduce(nmax[:, s, 1:2], bank[2 + s][:, P:3 * P], AXX, ALU.max,
                                    negate=True).then_inc(s_mx, 1)
                if has[3]:
                    b, slot = k - 3, (q - 3) % U
                    v.wait_ge(s_rr, b + 1)
                    wait(v, s_scat[slot], (use if q == 3 else use - 1) * (16 * 2 * TPB))
                    for t in range(TPB):
                        last = v.tensor_scalar(xh[:, slot, t, :], x_row(b, t), mv[:, (q - 3) % 2, t, 0:1],
                                               rr_all[:, bass.ds(b, 1), 1, t], ALU.subtract, ALU.mult)
                    last.then_inc(s_xh, 1)
                if has[4]:
                    v.wait_ge(s_lg, b4 + 1)
                if has[2]:
                    v.wait_ge(s_y, b2 + 1)
                    for t in range(TPB):
                        last = v.scalar_tensor_tensor(
                            out=x_row(b2, t), in0=bank[5][:, t * P:(t + 1) * P], scalar=rinv[:, s2, t:t + 1],
                            in1=x_row(b2, t), op0=ALU.mult, op1=ALU.add)
                    last.then_inc(s_yr, 1)
                if has[5]:
                    v.wait_ge(s_rk, b5 + 1)
                    op(v.tensor_tensor(ohr[:], one_hots(b5), rkb.unsqueeze(2).to_broadcast([P, TPB, 2, E]), ALU.mult))
                if has[4]:
                    for t in range(TPB):
                        op(v.max(mx8[:, t, :], lgb[:, t, :]))
                pg.settle()
                if has[5]:
                    with nc.allow_low_precision(reason="whole numbers below 2**24"):
                        op(v.tensor_reduce(pos_all[:, bass.ds(b5 * TPB, TPB), :], ohr[:], AXX, ALU.add))
                        v.tensor_reduce(pos_i[:, q5], ohr[:], AXX, ALU.add).then_inc(s_pos, 1)
                if has[4]:
                    for t in range(TPB):
                        op(v.max_index(ix8[:, t, :], mx8[:, t, :], lgb[:, t, :]))
                    v.tensor_tensor(gd[:, bass.ds(b4 * TPB, TPB)], mx8[:, :, 1], mx8[:, :, 0],
                                    ALU.subtract).then_inc(s_lr, 1)
                if has[2]:
                    if not has[4]:
                        v.wait_ge(s_yr, b2 + 1)
                    for t in range(TPB):
                        op(v.bn_stats(st6[:, t, :], x_row(b2, t)))
                pg.settle()
                if has[4]:
                    op(v.tensor_tensor(one_hots(b4), iota_e[:].unsqueeze(1).unsqueeze(1).to_broadcast([P, TPB, 2, E]),
                                       ix8[:, :, 0:2].unsqueeze(3).to_broadcast([P, TPB, 2, E]), ALU.is_equal))
                if has[1]:
                    v.wait_ge(s_p, k)
                    op(v.reciprocal(rinv[:, (q - 1) % 2, :], rsum[:, (q - 1) % U, :]))
                if has[2]:
                    for t in range(TPB):
                        op(v.bn_aggr(mv[:, s2, t, :], st6[:, t, :]))
                pg.settle()
                if has[4]:
                    v.tensor_tensor(m_sum[:, s4], oh_all[:, bass.ds(b4 * TPB, TPB), 0, :],
                                    oh_all[:, bass.ds(b4 * TPB, TPB), 1, :], ALU.add).then_inc(s_oh, 1)
                if has[2]:
                    op(v.tensor_scalar(vv[:, s2, 0, :], mv[:, s2, :, 1], EPS_POST, None, ALU.add))
                    v.tensor_scalar(vv[:, s2, 1, :], mv[:, s2, :, 1], 1.0 + EPS_FFN, EPS_POST * EPS_FFN, ALU.mult,
                                    ALU.add).then_inc(s_vv, 1)

            PER_STEP = 1 + 2 + 1 + 2 + 2 + 1 + 1 + 2 + 1
            run_steps(v, attend_step, NB + 5, U, 8, 5, progress=pg, per_step=PER_STEP)

            v.sem_inc(s_gd, 1)
            v.wait_ge(s_tot, 1)
            ends = bank[7][:, 0:E]
            op(v.tensor_scalar(padf[:], ends, part[:], None, ALU.add))
            op(v.tensor_tensor(cnt[:], ends, ebase[:], ALU.subtract))
            pg.settle()
            op(v.tensor_copy(padp[:], padf[:]))
            op(v.tensor_tensor(full[:], cnt[:].unsqueeze(2).to_broadcast([P, E, NT]),
                               kP_iota[:].unsqueeze(1).to_broadcast([P, E, NT]), ALU.is_gt))
            pg.settle()
            v.sem_inc(s_pad, 1)
            op(v.tensor_reduce(tiles[:], full[:], AXX, ALU.add))
            pg.settle()
            op(v.tensor_tensor_scan(out=incl[:], data0=ones[:, 0:E], data1=tiles[:], initial=0.0,
                                    op0=ALU.mult, op1=ALU.add))
            pg.settle()
            op(v.tensor_tensor(tb0[:], incl[:], tiles[:], ALU.subtract))
            op(v.tensor_scalar(shift[:, E:E + 1], incl[:, E - 1:E], -float(P), float(DUMMY), ALU.mult, ALU.add))
            pg.settle()
            op(v.scalar_tensor_tensor(out=shift[:, 0:E], in0=tb0[:], scalar=-float(P), in1=ebase[:],
                                      op0=ALU.mult, op1=ALU.add))
            op(v.tensor_tensor(cmp[:], j_iota[:].unsqueeze(2).to_broadcast([1, NTILE, E]),
                               incl[0:1, :].unsqueeze(1).to_broadcast([1, NTILE, E]), ALU.is_ge))
            pg.settle()
            op(v.tensor_reduce(ej[:], cmp[:], AXX, ALU.add))
            pg.settle()
            op(v.tensor_tensor(cmp9[:], ej[:].unsqueeze(2).to_broadcast([1, NTILE, E + 1]),
                               e_iota[:].unsqueeze(1).to_broadcast([1, NTILE, E + 1]), ALU.is_equal))
            op(v.tensor_scalar(tab_e[:], ej[:], float(E - 1), None, ALU.min))
            pg.settle()
            op(v.tensor_tensor(cmp9[:], cmp9[:], shift[0:1, :].unsqueeze(1).to_broadcast([1, NTILE, E + 1]), ALU.mult))
            pg.settle()
            op(v.tensor_reduce(rowf[:], cmp9[:], AXX, ALU.add))
            pg.settle()
            op(v.scalar_tensor_tensor(out=tab_row[:], in0=j_iota[:], scalar=float(P), in1=rowf[:],
                                      op0=ALU.mult, op1=ALU.add))
            pg.settle()
            v.sem_inc(s_tab, 1)

            def late_routing():
                op(v.tensor_tensor(ohs[:], oh_all[:].rearrange("p t k e -> p (t k) e"),
                                   shift[:, 0:E].unsqueeze(1).to_broadcast([P, NT * 2, E]), ALU.mult))
                v.wait_ge(s_ge, 1)
                op(v.tensor_scalar(gd[:], gates[:, :, 1], 1.0, None, ALU.add))
                pg.settle()
                op(v.tensor_reduce(yf[:], ohs[:], AXX, ALU.add))
                op(v.reciprocal(gates[:, :, 0], gd[:]))
                pg.settle()
                op(v.tensor_tensor(ypos[:].rearrange("p t k -> p (t k)"), pos_all[:].rearrange("p t k -> p (t k)"),
                                   yf[:], ALU.subtract))
                op(v.tensor_tensor(gates[:, :, 1], gates[:, :, 1], gates[:, :, 0], ALU.mult))
                pg.settle()
                v.sem_inc(s_gates, 1)
            late_routing()

            v.wait_ge(s_go, 16)

            def ffn_step(k, q, use, known):
                if known is None or known < NTILE:
                    e = v.value_load(tab_e[0:1, bass.ds(k, 1)], min_val=0, max_val=E - 1)
                    wait(v, s_h, k - 1)
                    v.tensor_copy(w1c[:, q % 2, :], w1T[:, bass.ds(e, 1), :].rearrange("p a h -> p (a h)")
                                  ).then_inc(s_w1s, 1)
                if known is None or 0 <= known - 2 < NTILE:
                    j, s, slot = k - 2, q % 2, (q - 2) % XR
                    e = v.value_load(tab_e[0:1, bass.ds(j, 1)], min_val=0, max_val=E - 1)
                    v.wait_ge(s_yy, j + 1)
                    wait(v, s_yo[slot], (use if q >= 2 else use - 1) * 16)
                    v.tensor_tensor(ysb[:, slot, :], bank[4 + s][:, 0:P],
                                    b2_bc[:, bass.ds(e, 1), :].rearrange("p a c -> p (a c)"), ALU.add
                                    ).then_inc(s_ys, 1)
            run_steps(v, ffn_step, NTILE + 2, XR, 6, 2)

            def comb_step(b, q, use, known):
                s = q % 2
                for t in range(TPB):
                    op(v.tensor_scalar(acc[:, s, t, :], x_all[:, bass.ds(b * TPB + t, 1), :].rearrange("p a c -> p (a c)"),
                                       rr_all[:, bass.ds(b, 1), 0, t], None, ALU.mult))
                pg.settle()
                v.wait_ge(s_gy[s], (use * 2 + q // 2) * 64 + 64)
                for c in range(2):
                    for t in range(TPB):
                        base = acc[:, s, t, :]
                        op(v.scalar_tensor_tensor(
                            out=acc[:, s, t, :], in0=gy[:, s, t, c, :],
                            scalar=gates[:, bass.ds(b * TPB + t, 1), c], in1=base, op0=ALU.mult, op1=ALU.add))
                    pg.settle()
                v.sem_inc(s_comb, 1)
                for t in range(TPB):
                    op(v.bn_stats(st7[:, t, :], acc[:, s, t, :]))
                pg.settle()
                own_wait(v, s_own_dve)
                for t in range(TPB):
                    op(v.bn_aggr(mv7[:, t, :], st7[:, t, :]))
                pg.settle()
                op(v.tensor_scalar(v7[:], mv7[:, :, 1], EPS_POST, None, ALU.add))
                pg.settle()
                rsqrt(r7[:], v7[:], t7i[:], t7[:])
                wait(v, s_out[q], use * 16)
                v.tensor_scalar(osb[:, q, 0, :], acc[:, s, 0, :], mv7[:, 0, 0:1], r7[:, 0:1], ALU.subtract, ALU.mult)
                v.tensor_scalar(osb[:, q, 1, :], acc[:, s, 1, :], mv7[:, 1, 0:1], r7[:, 1:2], ALU.subtract,
                                ALU.mult).then_inc(s_os, 1)
            run_steps(v, comb_step, NB, 4, 4, 0, progress=pg, per_step=11 + RSQRT_OPS)


NAMES = ("x", "W_attn", "W_proj", "lora_attn_A", "lora_attn_B", "lora_proj_A", "lora_proj_B", "bn_gamma", "bn_beta")
FFN_NAMES = ("router_ln_scale", "router_ln_bias", "router_w", "router_b", "expert_ln_scale", "expert_ln_bias",
             "w1", "b1", "w2", "b2")


def kernel(**inputs):
    import numpy as np
    import concourse.bacc as bacc
    from concourse.bass_utils import run_bass_kernel_spmd

    nc = bacc.Bacc("TRN2", target_bir_lowering=False, num_devices=1)
    arrays, args = {}, []
    for name in ["L0_attn_" + n for n in NAMES] + ["L0_ffn_" + n for n in FFN_NAMES]:
        a = np.ascontiguousarray(inputs[name])
        arrays[name] = a
        args.append(nc.dram_tensor(name, a.shape, mybir.dt.from_np(a.dtype), kind="ExternalInput").ap())
    shape = inputs["L0_attn_x"].shape
    out = nc.dram_tensor("out", shape, F32, kind="ExternalOutput").ap()
    build(nc, *args, out)
    r = run_bass_kernel_spmd(nc, [arrays], core_ids=[0])
    return r.results[0]["out"]
```

```python
from contextlib import ExitStack

import concourse.bass as bass
from concourse import mybir

F32 = mybir.dt.float32
BF16 = mybir.dt.bfloat16
F16 = mybir.dt.float16
I32 = mybir.dt.int32
U32 = mybir.dt.uint32
ALU = mybir.AluOpType
ACT = mybir.ActivationFunctionType
AXX = mybir.AxisListType.X

P = 128
MASKED = -1e30
EPS_BN = 1e-5
EPS_POST = 1e-5
EPS_FFN = 1e-6


class Progress:

    def __init__(self, eng, sem):
        self.eng, self.sem, self.base, self.n = eng, sem, 0, 0

    def did(self, ins):
        ins.then_inc(self.sem, 1)
        self.n += 1

    def settle(self):
        self.eng.wait_ge(self.sem, self.base + self.n)


def wait(eng, sem, value):
    if isinstance(value, int) and value <= 0:
        return
    eng.wait_ge(sem, value)


def run_steps(eng, step, total, unroll, front, back, progress=None, per_loop=0):
    loops = (total - front - back) // unroll
    for k in range(front):
        step(k, k % unroll, k // unroll, k)
    if loops:
        start = progress.n if progress else 0
        with eng.Fori(0, loops) as i:
            if progress:
                progress.base = eng.snap(i * per_loop)
            for j in range(front, front + unroll):
                step(eng.snap(i * unroll + j), j % unroll, eng.snap(i + j // unroll), None)
            if progress:
                assert progress.n - start == per_loop, (progress.n - start, per_loop)
        if progress:
            progress.base, progress.n = 0, start + loops * per_loop
    for k in range(front + loops * unroll, total):
        step(k, k % unroll, k // unroll, k)


def build(nc, x, w_attn, w_proj, la_a, la_b, lp_a, lp_b, gamma, beta, r_ls, r_lb, r_w, r_b,
          e_ls, e_lb, w1, b1, w2, b2, out):
    NB, T, C = x.shape
    E, H, _ = w1.shape
    R = la_a.shape[1]
    HC = H // P
    NTOK = NB * T
    NT = NTOK // P
    TPB = T // P
    CAP = NTOK + P
    DUMMY = E * CAP
    NB0 = 22
    NTILE0 = 2 * NB0 * TPB + E - 1
    NTILE = 2 * NT + 2 * (E - 1)
    NPART = E + 1
    assert C == P and TPB == 2
    assert NTILE % 2 == 0 and NTILE <= 2 * P and NTILE - NTILE0 >= 2 * NB0

    queues = [nc.dram_tensor(f"queue{g}", [DUMMY + E * P, P], F32, kind="Internal").ap() for g in range(2)]
    yrows = nc.dram_tensor("yrows", [NTILE * P, P], F32, kind="Internal").ap()

    with ExitStack() as ctx:
        def sb(name, shape, dt=F32):
            return ctx.enter_context(nc.sbuf_tensor(name, shape, dt))

        def sem(name):
            return ctx.enter_context(nc.semaphore(name))

        bank = [ctx.enter_context(nc.psum_tensor(f"bank{i}", [P, 512], F32)) for i in range(8)]

        xT = sb("xT", [P, NTOK])
        x_all = sb("x_all", [P, NT, P])
        w1T = sb("w1T", [P, E, H])
        w2T = sb("w2T", [P, E, HC, P])
        b2_bc = sb("b2_bc", [P, E * P])
        b2p = sb("b2p", [P, 3, E * P], BF16)
        b2_3 = sb("b2_3", [P, E, P], BF16)
        oh_all = sb("oh_all", [P, NT, 2, E])
        pos_all = sb("pos_all", [P, NT, 2], I32)
        gates = sb("gates", [P, NT, 2])
        ypos = sb("ypos", [P, NT, 2], I32)

        def carver(region):
            used = [0]

            def carve(shape):
                n, at = 1, used[0]
                for d in shape[1:]:
                    n *= d
                used[0] += n
                assert used[0] <= region.shape[1]
                names = "abcd"[:len(shape) - 1]
                return region[:, at:at + n].rearrange(f"p ({' '.join(names)}) -> p {' '.join(names)}",
                                                      **dict(zip(names, shape[1:])))
            return carve

        late = carver(xT)

        ident = sb("ident", [P, P])
        ident_b = sb("ident_b", [P, P], BF16)
        mask_b = sb("mask_b", [P, P], BF16)
        before = sb("before", [P, P], F16)
        not_before = sb("not_before", [P, P], F16)
        ones_h = sb("ones_h", [P, P], F16)
        ones = sb("ones", [P, P])
        ones_b = sb("ones_b", [P, P], BF16)
        zeros = sb("zeros", [P, P])
        inv_c = sb("inv_c", [1, P])
        iota_e = sb("iota_e", [P, E])
        part = sb("part", [P, 1])
        one_col = sb("one_col", [P, 1])

        s_const = sem("s_const")
        s_mat, s_par, s_go = sem("s_mat"), sem("s_par"), sem("s_go")
        N_MAT, N_PARAM = 6, 6
        s_dve, s_pool = sem("s_dve"), sem("s_pool")

        CH, RING = 4, 4
        NCH = NT // CH
        xin = sb("xin", [P, RING, CH, 132])
        s_xin = [sem(f"s_xin{i}") for i in range(RING)]
        s_t1, s_cp1, s_ev = sem("s_t1"), sem("s_cp1"), sem("s_ev")
        x_chunks = x.rearrange("b t c -> (b t) c").rearrange("(n j p) c -> n p j c", j=CH, p=P)

        wa = sb("wa", [P, 3, P])
        wp = sb("wp", [P, P])
        aA, aB = sb("aA", [P, R]), sb("aB", [R, 3 * P])
        pA, pB = sb("pA", [P, R]), sb("pB", [R, P])
        gb = sb("gb", [P, 2, 3])
        rls, rlb = sb("rls", [P, 1]), sb("rlb", [P, 1])
        rwT, rb = sb("rwT", [P, E]), sb("rb", [1, E])
        aAT, pAT = sb("aAT", [R, P]), sb("pAT", [R, P])
        wm = sb("wm", [P, 3, P])
        wmT = sb("wmT", [P, 3 * P])
        wn = sb("wn", [P, 3, P])
        cov = sb("cov", [P, P + 1])
        scr3 = sb("scr3", [P, 3, P])
        bn = sb("bn", [P, 5, 3])
        s_bnv, s_bnl, s_bnr, s_cv = [sem(n) for n in ("s_bnv", "s_bnl", "s_bnr", "s_cv")]
        wpmT = sb("wpmT", [P, P])
        wp2T = sb("wp2T", [P, P])
        tv_bc = sb("tv_bc", [P, P])
        MT = sb("MT", [P, P])
        u_z = sb("u_z", [P, 1])
        wvvT = sb("wvvT", [P, P])
        cv = sb("cv", [P, P])
        cv3 = sb("cv3", [P, P], BF16)
        cvp = sb("cvp", [P, 3, P], BF16)
        rl_bc = sb("rl_bc", [P, P])
        rl_d = sb("rl_d", [P, 1])
        RW = sb("RW", [P, E])

        w_rows = sb("w_rows", [P, 2 * E * H])
        w2n = w_rows[:, 0:E * H].rearrange("p (e h) -> p e h", e=E)
        w1n = w_rows[:, E * H:2 * E * H].rearrange("p (e k d) -> p e k d", e=E, k=HC)
        LATE_W = 3
        EARLY = 2 * E - LATE_W
        after_weights = carver(w_rows[:, 0:(2 * E - LATE_W) * H])

        FIRST_W = 3
        WEIGHTS_AFTER_CHUNK = {5: 0, 6: 1, 7: 2}

        def weights_bank(g):
            return 4 + g % 3 if FIRST_W <= g < EARLY else 6

        def copied_before(g):
            return max([n + 1 for n in range(g) if weights_bank(n) == weights_bank(g)], default=0)

        b1r = sb("b1r", [E * HC, P])
        b1c = sb("b1c", [P, E * HC])
        ls_bc, ld_bc = sb("ls_bc", [P, E * P]), sb("ld_bc", [P, E * P])
        w1s = sb("w1s", [P, HC, P])
        w1k = sb("w1k", [P, HC])
        s_w = [sem("s_w0"), sem("s_w1")]
        s_b1, s_b1t, s_b1c, s_ls, s_ld, s_w1p, s_wt, s_wc = [sem(n) for n in (
            "s_b1", "s_b1t", "s_b1c", "s_ls", "s_ld", "s_w1p", "s_wt", "s_wc")]

        U = 4
        xTs = after_weights([P, 2, T])
        zT = after_weights([P, 2, T])
        vs = after_weights([P, U, TPB, P])
        nmax, rsum = sb("nmax", [P, 2, TPB]), sb("rsum", [P, U, TPB])
        rinv = sb("rinv", [P, 2, TPB])
        pr = after_weights([P, 2, 3, P])
        prT = after_weights([P, 2, 3, P])
        st6, mv = sb("st6", [P, TPB, 6]), sb("mv", [P, 2, TPB, 2])
        vv = sb("vv", [P, 2, 2, TPB])
        lnv = sb("lnv", [P, 2, 2, TPB])
        rr_all = sb("rr_all", [P, NB, 2, TPB])
        ROWS = 8
        SCAT = 16 * 2 * TPB
        xh = after_weights([P, ROWS, TPB, P])
        xhT = after_weights([P, 2, TPB, P])
        mx8 = sb("mx8", [P, TPB, 8])
        ix8 = sb("ix8", [P, TPB, 8], U32)
        m_sum = sb("m_sum", [P, 2, TPB, E], F16)
        base_h = sb("base_h", [P, TPB, E], F16)
        ohr = sb("ohr", [P, TPB, 2, E])
        pos_i = sb("pos_i", [P, ROWS, TPB, 2], I32)
        (s_xts, s_z, s_v, s_zs, s_vs, s_sc, s_mx, s_p, s_pt, s_pts, s_y, s_xh, s_xht, s_xhts,
         s_lg, s_oh, s_rk, s_pos, s_vv, s_ln, s_rr, s_yr, s_lr) = [sem(n) for n in (
            "s_xts", "s_z", "s_v", "s_zs", "s_vs", "s_sc", "s_mx", "s_p", "s_pt", "s_pts", "s_y", "s_xh",
            "s_xht", "s_xhts", "s_lg", "s_oh", "s_rk", "s_pos", "s_vv", "s_ln", "s_rr", "s_yr", "s_lr")]
        s_scat = [sem(f"s_scat{i}") for i in range(ROWS)]

        n0_h = sb("n0_h", [P, E], F16)
        n0 = sb("n0", [P, E])
        base = sb("base", [P, 2, NPART])
        tiles_i, tiles_s = sb("tiles_i", [P, 2, E], I32), sb("tiles_s", [P, 2, E], I32)
        tiles = sb("tiles", [P, 2, E])
        start = sb("start", [P, 2, NPART])
        look = sb("look", [P, 2, 2 * NPART])
        g_iota = sb("g_iota", [P, 2 * NPART])
        j_iota = sb("j_iota", [P, 2])
        cmp = sb("cmp", [P, 2, 2 * NPART])
        part_j = sb("part_j", [P, 2])
        pick = sb("pick", [P, 2, 2 * NPART])
        picked = sb("picked", [P, 2, 2, 2 * NPART])
        tab_p = sb("tab_p", [P, 2, 2])
        tab = sb("tab", [1, 2, NTILE], I32)
        tab_row, tab_e = tab[:, 0, :], tab[:, 1, :]
        padp = sb("padp", [P, E], I32)
        ends_i = sb("ends_i", [1, E], I32)
        ohs = late([P, NT * 2, E])
        yf = sb("yf", [P, NT * 2])
        gd = sb("gd", [P, NT])
        gsum = sb("gsum", [P, NT])
        s_n0, s_tot, s_tabp, s_tabt, s_tab, s_pad, s_zero, s_gd, s_ge, s_n0t = [sem(n) for n in (
            "s_n0", "s_tot", "s_tabp", "s_tabt", "s_tab", "s_pad", "s_zero", "s_gd", "s_ge", "s_n0t")]
        s_n0r = sem("s_n0r")
        COUNT0 = NB0 + 8
        s_padd = [sem("s_padd0"), sem("s_padd1")]
        s_ypos = sem("s_ypos")

        XR = 4
        xg = late([P, XR, P])
        xgT = late([P, 2, P])
        w1c = late([P, XR, H])
        hs = late([P, 2, HC, P])
        ysb = late([P, XR, P])
        s_xg = [sem(f"s_xg{i}") for i in range(XR)]
        s_yo = [sem(f"s_yo{i}") for i in range(XR)]
        s_gt, s_gts, s_w1s, s_h, s_hs, s_yy, s_ys = [sem(n) for n in (
            "s_gt", "s_gts", "s_w1s", "s_h", "s_hs", "s_yy", "s_ys")]

        gy = late([P, U, TPB, 2, P])
        yidx = sb("yidx", [P, U, TPB, 2], I32)
        st7, mv7 = sb("st7", [P, TPB, 6]), sb("mv7", [P, TPB, 2])
        neg_mv = sb("neg_mv", [P, NT, 2])
        eps_col, eps_bn = sb("eps_col", [P, 1]), sb("eps_bn", [P, 1])
        ln7, r7 = sb("ln7", [P, 2, TPB]), sb("r7", [P, 2, TPB])
        sh7 = sb("sh7", [P, 2, TPB])
        ln70, r70, sh70 = [sb(n, [P, NB0 * TPB]) for n in ("ln70", "r70", "sh70")]
        s_sh70 = sem("s_sh70")
        s_comb, s_mv, s_ln7, s_r7, s_sh7, s_os, s_out = [sem(n) for n in (
            "s_comb", "s_mv", "s_ln7", "s_r7", "s_sh7", "s_os", "s_out")]
        s_gy = [sem(f"s_gy{i}") for i in range(U)]

        s_own_dve, s_own_pool = sem("s_own_dve"), sem("s_own_pool")

        def own_wait(eng, s_own):
            eng.sem_inc(s_own, 1)

        out_v = out.rearrange("b (j p) c -> b p j c", p=P)

        s_x1, s_b2 = sem("s_x1"), sem("s_b2")
        zero_col = sb("zero_col", [P, 1])

        def x_row(b, t):
            return x_all[:, bass.ds(b * TPB + t, 1), :].rearrange("p a c -> p (a c)")

        block = ctx.enter_context(nc.Block())

        @block.sync
        def _(sp):
            def load_chunk(c, slot):
                sp.dma_start(xin[:, slot, :, 0:P], x_chunks[c]).then_inc(s_xin[slot], 16)

            def load_expert(e, slot, use):
                wait(sp, s_w[slot], use * 32)
                sp.dma_start(w1n[:, bass.ds(e, 1)].rearrange("p a k d -> p (a k) d"),
                             w1[e].rearrange("(k p) d -> p k d", p=P)).then_inc(s_w[slot], 16)
                sp.dma_start(w2n[:, bass.ds(e, 1)].rearrange("p a h -> p (a h)"), w2[e]).then_inc(s_w[slot], 16)

            for c in range(RING):
                load_chunk(c, c)
            for dst, src in ((aA[:], la_a), (pA[:], lp_a), (aB[:], la_b), (pB[:], lp_b), (wp[:], w_proj),
                             (wa[:], w_attn.rearrange("(i a) c -> i a c", a=3))):
                sp.dma_start(dst, src).then_inc(s_mat, 16)
            def load_ahead(k, j, use, known):
                if known is not None and known < RING:
                    return
                sp.wait_ge(s_t1, k - RING + 1)
                sp.wait_ge(s_cp1, k - RING + 1)
                load_chunk(k, j)
                if known is not None:
                    load_expert(j, j % 2, j // 2)
                elif j < 2:
                    load_expert(sp.snap(use * 2 + j), j, use)
            run_steps(sp, load_ahead, NCH, RING, 2 * RING, 0)
            sp.dma_start(b2_bc[:], b2.rearrange("e d -> (e d)").partition_broadcast(P)).then_inc(s_go, 16)
            wait(sp, s_const, 1)
            for queue in queues:
                sp.dma_start(queue[DUMMY:DUMMY + E * P, :].rearrange("(a p) c -> p a c", p=P),
                             zeros[:, :].unsqueeze(1).to_broadcast([P, E, P])).then_inc(s_zero, 16)

            for g, (first, last, n_batch) in enumerate(((0, NTILE0, NB0), (NTILE0, NTILE, NB))):
                queue = queues[g]
                if g == 0:
                    sp.wait_ge(s_pad, 1)
                    for e in range(E):
                        end = sp.value_load(ends_i[0:1, e:e + 1], min_val=e * CAP, max_val=e * CAP + NTOK)
                        sp.dma_start(queue[bass.ds(end, P), :], zeros[:]).then_inc(s_padd[0], 16)
                for q in range(ROWS):
                    sp.wait_ge(s_scat[q], SCAT * len(range(q, n_batch, ROWS)))
                sp.wait_ge(s_padd[g], 16 * E)
                sp.wait_ge(s_zero, 32)
                sp.wait_ge(s_tab, 1)

                def load_rows(n, slot, use, known):
                    j = n + first
                    wait(sp, s_gt, j - XR + 1)
                    row = sp.value_load(tab_row[0:1, bass.ds(j, 1)], min_val=0, max_val=DUMMY + (E - 1) * P)
                    sp.dma_start(xg[:, (slot + first) % XR], queue[bass.ds(row, P), :]
                                 ).then_inc(s_xg[(slot + first) % XR], 16)
                run_steps(sp, load_rows, last - first, XR, XR if g == 0 else 0, 0)

            with sp.Fori(0, NB) as b:
                sp.wait_ge(s_os, b + 1)
                sp.dma_start(out_v[b], x_all[:, bass.ds(b * TPB, TPB), :]).then_inc(s_out, 16)
            sp.wait_ge(s_out, 16 * NB)

        @block.gpsimd
        def _(pool):
            pg = Progress(pool, s_pool)
            pg.did(pool.memset(ones[:], 1.0))
            pg.did(pool.memset(ones_b[:], 1.0))
            pg.did(pool.memset(ones_h[:], 1.0))
            pg.did(pool.memset(cv3[:], 0.0))
            pg.did(pool.memset(b2_3[:], 0.0))
            pg.did(pool.iota(base_h[:], [[0, TPB], [CAP // P, E]], base=0, channel_multiplier=0,
                             allow_small_or_imprecise_dtypes=True))
            pg.did(pool.memset(zeros[:], 0.0))
            pg.did(pool.memset(inv_c[:], 1.0 / C))
            pg.did(pool.memset(one_col[:], 1.0))
            pg.did(pool.memset(zero_col[:], 0.0))
            for s in range(RING):
                pg.did(pool.memset(xin[:, s, :, P:P + 1], 1.0))
            pg.did(pool.memset(mask_b[:], 0.0))
            pg.did(pool.iota(iota_e[:], [[1, E]], base=0, channel_multiplier=0, allow_small_or_imprecise_dtypes=True))
            pg.did(pool.iota(g_iota[:], [[1, 2 * NPART]], base=1, channel_multiplier=0,
                             allow_small_or_imprecise_dtypes=True))
            for g in range(2):
                pg.did(pool.iota(look[:, 1, g * NPART:g * NPART + E], [[1, E]], base=0, channel_multiplier=0,
                                 allow_small_or_imprecise_dtypes=True))
                pg.did(pool.memset(look[:, 1, g * NPART + E:(g + 1) * NPART], E - 1.0))
                pg.did(pool.memset(base[:, g, E:NPART], float(DUMMY)))
                pg.did(pool.memset(start[:, g, 0:1], float(g * NTILE0)))
            pg.did(pool.memset(eps_col[:], EPS_POST))
            pg.did(pool.memset(eps_bn[:], EPS_BN))
            pg.did(pool.iota(j_iota[:], [[P, 2]], base=0, channel_multiplier=1, allow_small_or_imprecise_dtypes=True))
            pg.did(pool.iota(part[:], [[0, 1]], base=0, channel_multiplier=1, allow_small_or_imprecise_dtypes=True))
            pg.did(pool.iota(base[:, 0, 0:E], [[CAP, E]], base=0, channel_multiplier=0,
                             allow_small_or_imprecise_dtypes=True))
            pg.settle()
            pg.did(pool.affine_select(out=ident[:], in_=ones[:], pattern=[[-1, P]], compare_op=ALU.is_equal,
                                      fill=0.0, base=0, channel_multiplier=1))
            pg.did(pool.affine_select(out=ident_b[:], in_=ones_b[:], pattern=[[-1, P]], compare_op=ALU.is_equal,
                                      fill=0.0, base=0, channel_multiplier=1))
            pg.did(pool.affine_select(out=mask_b[:], in_=mask_b[:], pattern=[[-1, P]], compare_op=ALU.is_ge,
                                      fill=MASKED, base=0, channel_multiplier=1))
            pg.did(pool.affine_select(out=before[:], in_=ones_h[:], pattern=[[1, P]], compare_op=ALU.is_gt,
                                      fill=0.0, base=0, channel_multiplier=-1))
            pg.did(pool.affine_select(out=not_before[:], in_=ones_h[:], pattern=[[-1, P]], compare_op=ALU.is_ge,
                                      fill=0.0, base=0, channel_multiplier=1))
            pg.settle()
            pool.sem_inc(s_const, 1)
            with pool.Fori(0, NCH // RING) as i:
                for j in range(RING):
                    pool.wait_ge(s_xin[j], i * 16 + 16)
                    pool.tensor_copy(x_all[:, bass.ds(i * (RING * CH) + j * CH, CH), :],
                                     xin[:, j, :, 0:P]).then_inc(s_cp1, 1)
            pool.wait_ge(s_go, 16)
            for n in range(3):
                pg.did(pool.tensor_copy(b2p[:, n, :], b2_bc[:]))
                pg.settle()
                row = slice(32 * n, 32 * n + 1)
                pg.did(pool.tensor_copy(b2_3[row].rearrange("p e d -> p (e d)"), b2p[row, n, :]))
                pg.settle()
                if n < 2:
                    pg.did(pool.tensor_tensor(b2_bc[:], b2_bc[:], b2p[:, n, :], ALU.subtract))
                pg.settle()
            pool.sem_inc(s_b2, 1)
            def scatter_step(b, q, queue):
                wait(pool, s_pos, b + 1)
                own_wait(pool, s_own_pool)
                for t in range(TPB):
                    for c in range(2):
                        pool.indirect_dma_start(
                            out=queue, out_offset=bass.IndirectOffsetOnAxis(pos_i[:, q, t, c:c + 1], 0),
                            in_=xh[:, q, t, :], in_offset=None).then_inc(s_scat[q], 16)
            for g, (first, last) in enumerate(((0, NB0), (NB0, NB))):
                run_steps(pool, lambda n, q, use, known: scatter_step(n + first, (q + first) % ROWS, queues[g]),
                          last - first, ROWS, 0, 0)
            pool.wait_ge(s_pad, 2)
            for e in range(E):
                pool.indirect_dma_start(out=queues[1], out_offset=bass.IndirectOffsetOnAxis(padp[:, e:e + 1], 0),
                                        in_=zeros[:], in_offset=None).then_inc(s_padd[1], 16)
            def gather_step(b, r, n_tiles):
                wait(pool, s_comb, b - U + 1)
                if not isinstance(b, int):
                    own_wait(pool, s_own_pool)
                for t in range(TPB):
                    for c in range(2):
                        pool.indirect_dma_start(
                            out=gy[:, r, t, c, :], out_offset=None, in_=yrows[0:n_tiles * P, :],
                            in_offset=bass.IndirectOffsetOnAxis(yidx[:, r, t, c:c + 1], 0)).then_inc(s_gy[r], 16)

            for first, last, n_tiles in ((0, NB0, NTILE0), (NB0, NB, NTILE)):
                for q in range(XR):
                    pool.wait_ge(s_yo[q], 16 * len(range(q, n_tiles, XR)))
                if first == 0:
                    pool.wait_ge(s_ypos, 1)
                run_steps(pool, lambda n, q, use, known: gather_step(n + first, (q + first) % U, n_tiles),
                          last - first, U, U if first == 0 else 0, 0)

        s_gram = sem("s_gram")
        s_fold_pe, s_fold_dve = sem("s_fold_pe"), sem("s_fold_dve")

        @block.tensor
        def _(pe):
            mm, tr = pe.matmul, pe.transpose
            pe.wait_ge(s_const, 1)
            gram = bank[7][:, 0:P + 1]

            def gram_zero(start):
                return mm(gram, zeros[:], xin[:, 0, 0, 0:P + 1], start=start, stop=not start)

            pe.wait_ge(s_xin[0], 16)
            gram_zero(True)

            def round_opens(r):
                wait(pe, s_fold_dve, r if r < 4 else r + 1)

            def fold_round(r):
                round_opens(r)
                if r == 0:
                    pe.wait_ge(s_mat, 16 * N_MAT)
                    tr(bank[5][0:R, 0:P], aA[:], ident[:])
                    last = tr(bank[5][0:R, P:2 * P], pA[:], ident[:])
                elif r == 1:
                    mm(bank[3][:, 0:3 * P], aAT[:], aB[:], start=True, stop=True)
                    mm(bank[2][:, 0:P], wp[:], ident[:], start=True, stop=False)
                    last = mm(bank[2][:, 0:P], pB[:], pAT[:], start=False, stop=True)
                elif r == 2:
                    for a in range(3):
                        tr(bank[4][:, a * P:(a + 1) * P], wm[:, a, :], ident[:])
                    last = mm(bank[2][:, P:2 * P], wp[:], wpmT[:], start=True, stop=True)
                elif r == 3:
                    for g in range(3):
                        last = tr(bank[5][:, g * P:(g + 1) * P], wmT[:, g * P:(g + 1) * P], ident[:])
                elif r == 4:
                    for g in range(3):
                        last = mm(bank[3][:, g * (P + 1):(g + 1) * (P + 1)], wmT[:, g * P:(g + 1) * P], cov[:],
                                  start=True, stop=True)
                else:
                    pe.wait_ge(s_par, 16 * N_PARAM)
                    mm(bank[2][:, 0:P], wn[:, 0, :], wn[:, 1, :], start=True, stop=True)
                    mm(bank[2][:, P:P + 1], wn[:, 1, :], bn[:, 2, 0:1], start=True, stop=True)
                    mm(bank[3][:, 0:P], wn[:, 2, :], wp2T[:], start=True, stop=True)
                    mm(bank[3][:, P:2 * P], tv_bc[:], wp2T[:], start=True, stop=True)
                    mm(bank[3][:, 2 * P:2 * P + E], rl_bc[:], rwT[:], start=True, stop=False)
                    last = mm(bank[3][:, 2 * P:2 * P + E], inv_c[:], rb[:], start=False, stop=True)
                last.then_inc(s_fold_pe, 1)

            ROUND_AFTER_CHUNK = {2: 0, 4: 1, 6: 2, 7: 3}

            def transpose_weights(first, last):
                for g in range(first, last):
                    pe.wait_ge(s_w[g % 2], 32 * (g % E // 2 + 1))
                    if g >= E:
                        pe.wait_ge(s_w1p, g - E + 1)
                    wait(pe, s_wc, copied_before(g))
                    for h in range(HC):
                        done = tr(bank[weights_bank(g)][:, h * P:(h + 1) * P],
                                  w2n[:, g, h * P:(h + 1) * P] if g < E else w1n[:, g - E, h, :], ident[:])
                    done.then_inc(s_wt, 1)

            def chunk_step(k, q, use, known):
                pe.wait_ge(s_xin[q], use * 16 + 16)
                wait(pe, s_ev, k - 1)
                for t in range(CH):
                    tr(bank[q % 2][:, t * P:(t + 1) * P], xin[:, q, t, 0:P], ident[:])
                for t in range(CH):
                    last = mm(gram, xin[:, q, t, 0:P], xin[:, q, t, 0:P + 1], start=False, stop=False)
                last.then_inc(s_t1, 1)
                if known == 0:
                    pe.wait_ge(s_b1, 16)
                    tr(bank[6][:, 0:E * HC], b1r[:], ident[0:E * HC, 0:E * HC]).then_inc(s_b1t, 1)
                if known in ROUND_AFTER_CHUNK:
                    fold_round(ROUND_AFTER_CHUNK[known])
                if known in WEIGHTS_AFTER_CHUNK:
                    transpose_weights(WEIGHTS_AFTER_CHUNK[known], WEIGHTS_AFTER_CHUNK[known] + 1)
            run_steps(pe, chunk_step, NCH, RING, 2 * RING, 0)
            gram_zero(False).then_inc(s_gram, 1)

            pe.wait_ge(s_fold_dve, 4)
            transpose_weights(FIRST_W, FIRST_W + 1)
            fold_round(4)
            transpose_weights(FIRST_W + 1, EARLY - 2)
            fold_round(5)
            transpose_weights(EARLY - 2, EARLY)
            pe.wait_ge(s_ev, NCH)
            pe.wait_ge(s_wc, EARLY)
            round_opens(6)

            tally = bank[7][:, 0:TPB * E]
            logits = bank[5][:, T:T + TPB * E]

            def add(t, weights, m, **kw):
                return mm(bank[7][:, t * E:(t + 1) * E], weights[:], m, skip_group_check=True, **kw)

            mm(tally, ones_h[:], base_h[:].rearrange("p t e -> p (t e)"), start=True, stop=False,
               skip_group_check=True)

            def rank_rest(s):
                for t in range(TPB):
                    add(t, not_before, m_sum[:, s, t, :], start=False, stop=False)
                return add(0, ones_h, m_sum[:, s, 1, :], start=False, stop=False)

            def z_and_v(b, s, q):
                pe.wait_ge(s_xts, b + 1)
                wait(pe, s_zs, b)
                mm(bank[0][:, 0:T], MT[:], xTs[:, s, :], start=True, stop=True).then_inc(s_z, 1)
                if isinstance(b, int) and b == 0:
                    pe.wait_ge(s_cv, 1)
                wait(pe, s_vs, b)
                for t in range(TPB):
                    o = bank[1][:, t * P:(t + 1) * P]
                    mm(o, ones_b[:], cv3[:], start=True, stop=False)
                    last = mm(o, xTs[:, s, t * P:(t + 1) * P], wvvT[:], start=False, stop=True)
                last.then_inc(s_v, 1)

            def scores(b, s):
                pe.wait_ge(s_zs, b + 1)
                wait(pe, s_p, b - 1)
                sc = bank[2 + s]
                mm(sc[:, 0:P], ident_b[:], mask_b[:], start=True, stop=False)
                mm(sc[:, 0:P], zT[:, s, 0:P], xTs[:, s, 0:P], start=False, stop=True)
                mm(sc[:, P:2 * P], zT[:, s, P:T], xTs[:, s, 0:P], start=True, stop=True)
                mm(sc[:, 2 * P:3 * P], ident_b[:], mask_b[:], start=True, stop=False)
                mm(sc[:, 2 * P:3 * P], zT[:, s, P:T], xTs[:, s, P:T], start=False, stop=True).then_inc(s_sc, 1)

            def attend_step(k, q, use, known):
                has = {d: known is None or 0 <= known - d < NB for d in (-1, 1, 3, 4)}
                if known == 0:
                    z_and_v(0, 0, 0)
                    scores(0, 0)
                if known is not None and known < LATE_W:
                    transpose_weights(EARLY + known, EARLY + known + 1)
                if known == LATE_W:
                    pe.wait_ge(s_wc, 2 * E)
                if has[1]:
                    b, s = k - 1, (q - 1) % 2
                    pe.wait_ge(s_p, b + 1)
                    wait(pe, s_pts, b)
                    for n in range(3):
                        last = tr(bank[4][:, n * P:(n + 1) * P], pr[:, s, n, :], ident[:])
                    last.then_inc(s_pt, 1)
                if has[-1]:
                    z_and_v(k + 1, (q + 1) % 2, q + 1)
                if has[3]:
                    b = k - 3
                    pe.wait_ge(s_xh, b + 1)
                    wait(pe, s_xhts, b)
                    if known == COUNT0 + 1:
                        pe.wait_ge(s_n0r, 1)
                    for t in range(TPB):
                        last = tr(bank[6][:, t * P:(t + 1) * P], xh[:, (q - 3) % ROWS, t, :], ident[:])
                    last.then_inc(s_xht, 1)
                if has[-1]:
                    scores(k + 1, (q + 1) % 2)
                if has[1]:
                    b, s = k - 1, (q - 1) % 2
                    pe.wait_ge(s_pts, b + 1)
                    pe.wait_ge(s_vs, b + 1)
                    wait(pe, s_yr, b)
                    wait(pe, s_lr, b - 2)
                    v0, v1 = vs[:, (q - 1) % U, 0, :], vs[:, (q - 1) % U, 1, :]
                    mm(bank[5][:, 0:P], prT[:, s, 0, :], v0, start=True, stop=True)
                    mm(bank[5][:, P:T], prT[:, s, 1, :], v0, start=True, stop=False)
                    mm(bank[5][:, P:T], prT[:, s, 2, :], v1, start=False, stop=True).then_inc(s_y, 1)
                if has[3]:
                    b, s = k - 3, (q - 3) % 2
                    pe.wait_ge(s_xhts, b + 1)
                    wait(pe, s_lr, b)
                    for t in range(TPB):
                        last = mm(logits[:, t * E:(t + 1) * E], xhT[:, s, t, :], RW[:],
                                  start=True, stop=True)
                    last.then_inc(s_lg, 1)
                if has[4]:
                    b, s = k - 4, q % 2
                    pe.wait_ge(s_oh, b + 1)
                    wait(pe, s_pos, b)
                    if known is None or known > 4:
                        rank_rest(1 - s)
                    add(0, before, m_sum[:, s, 0, :], start=False, stop=False)
                    add(1, ones_h, m_sum[:, s, 0, :], start=False, stop=False)
                    add(1, before, m_sum[:, s, 1, :], start=False, stop=False).then_inc(s_rk, 1)
                if known == COUNT0:
                    pe.wait_ge(s_n0, 1)
                    mm(bank[6][:, T:T + E], ones_h[:], n0_h[:], start=True, stop=True).then_inc(s_n0t, 1)
            run_steps(pe, attend_step, NB + 4, ROWS, 5, 4)
            pe.wait_ge(s_pos, NB)
            rank_rest((NB - 1) % 2).then_inc(s_tot, 1)
            pe.wait_ge(s_tabp, 1)
            for kind in range(2):
                for h in range(2):
                    last = mm(bank[4][0:1, (kind * 2 + h) * P:(kind * 2 + h + 1) * P], tab_p[:, h, kind:kind + 1],
                              ident[:], start=True, stop=True)
            last.then_inc(s_tabt, 1)

            pe.wait_ge(s_b2, 1)
            pe.wait_ge(s_tab, 1)

            def ffn_step(k, q, use, known):
                if known is None or known >= 2:
                    e = pe.value_load(tab_e[0:1, bass.ds(k - 2, 1)], min_val=0, max_val=E - 1)
                if known is None or known < NTILE:
                    pe.wait_ge(s_xg[q % XR], (use * 2 + q // XR) * 16 + 16)
                    wait(pe, s_gts, k - 1)
                    tr(bank[q % 2][:, 0:P], xg[:, q % XR, :], ident[:]).then_inc(s_gt, 1)
                if known is None or 0 <= known - 1 < NTILE:
                    j, s = k - 1, (q - 1) % 2
                    pe.wait_ge(s_gts, j + 1)
                    pe.wait_ge(s_w1s, j + 1)
                    wait(pe, s_hs, j - 1)
                    for h in range(HC):
                        last = mm(bank[2 + s][:, h * P:(h + 1) * P], w1c[:, (q - 1) % XR, h * P:(h + 1) * P],
                                  xgT[:, s, :], start=True, stop=True)
                    last.then_inc(s_h, 1)
                if known is None or 0 <= known - 2 < NTILE:
                    j, s = k - 2, q % 2
                    pe.wait_ge(s_hs, j + 1)
                    wait(pe, s_ys, j - 1)
                    mm(bank[4 + s][:, 0:P], ones_b[:], b2_3[:, bass.ds(e, 1), :].rearrange("p a d -> p (a d)"),
                       start=True, stop=False)
                    for h in range(HC):
                        last = mm(bank[4 + s][:, 0:P], hs[:, s, h, :],
                                  w2T[:, bass.ds(e, 1), h, :].rearrange("p a d -> p (a d)"),
                                  start=False, stop=(h == HC - 1))
                    last.then_inc(s_yy, 1)
            run_steps(pe, ffn_step, NTILE + 2, 2 * XR, 2 * XR, 2)

        @block.scalar
        def _(act):
            def cp(out_, in_, bias=0.0):
                return act.activation(out_, in_, ACT.Identity, bias=bias)

            act.preload_act_table_set("natural_log_exp_and_others")
            act.dma_start(b1r[:], b1.rearrange("e (k p) -> (e k) p", p=P)).then_inc(s_b1, 16)
            with nc.allow_non_contiguous_dma(reason="small parameters, transposed"):
                for dst, src in ((gb[:, 0, :], gamma.rearrange("(a p) -> p a", p=P)),
                                 (gb[:, 1, :], beta.rearrange("(a p) -> p a", p=P)),
                                 (rls[:], r_ls.unsqueeze(1)), (rlb[:], r_lb.unsqueeze(1)),
                                 (rb[:], r_b.unsqueeze(0)), (rwT[:], r_w.rearrange("e d -> d e"))):
                    act.dma_start(dst, src).then_inc(s_par, 16)
            act.dma_start(ls_bc[:], e_ls.rearrange("e d -> (e d)").partition_broadcast(P)).then_inc(s_ls, 16)
            act.dma_start(ld_bc[:], e_lb.rearrange("e d -> (e d)").partition_broadcast(P)).then_inc(s_ls, 16)
            act.wait_ge(s_const, 1)

            def copy_weights(g):
                act.wait_ge(s_wt, g + 1)
                dst = w2T[:, g].rearrange("p h d -> p (h d)") if g < E else w1T[:, g - E, :]
                cp(dst, bank[weights_bank(g)][:], bias=zero_col[:]).then_inc(s_wc, 1)

            def copy_chunk(c, q, use, known):
                act.wait_ge(s_t1, c + 1)
                cp(xT[:, bass.ds(c * (CH * P), CH * P)], bank[q][:]).then_inc(s_ev, 1)
                if known in WEIGHTS_AFTER_CHUNK:
                    copy_weights(WEIGHTS_AFTER_CHUNK[known])
            run_steps(act, copy_chunk, NCH, 2, 2 * RING, 0)

            for g in range(FIRST_W, EARLY):
                copy_weights(g)
                if g == FIRST_W + 2:
                    act.wait_ge(s_bnv, 1)
                    act.activation(bn[:, 3, :], bn[:, 0, :], ACT.Ln, bias=eps_bn[:]).then_inc(s_bnl, 1)
                    act.wait_ge(s_bnl, 1)
                    act.activation(bn[:, 1, :], bn[:, 3, :], ACT.Exp, scale=-0.5).then_inc(s_bnr, 1)

            act.wait_ge(s_fold_dve, 7)

            def copy_xT(b, s):
                wait(act, s_sc, b - 1)
                cp(xTs[:, s, :], xT[:, bass.ds(b * T, T)]).then_inc(s_xts, 1)

            def copy_z_v(b, q):
                act.wait_ge(s_z, b + 1)
                wait(act, s_sc, b - 1)
                cp(zT[:, q % 2, :], bank[0][:, 0:T], bias=u_z[:]).then_inc(s_zs, 1)
                act.wait_ge(s_v, b + 1)
                wait(act, s_y, b - U + 1)
                cp(vs[:, q % U].rearrange("p t c -> p (t c)"), bank[1][:, 0:T]).then_inc(s_vs, 1)

            def attend_step(k, q, use, known):
                has = {d: known is None or 0 <= known - d < NB for d in (-2, -1, 0, 1, 2, 3)}
                if known == 0:
                    copy_xT(0, 0)
                    copy_xT(1, 1)
                    copy_z_v(0, 0)
                if has[0]:
                    b, s = k, q % 2
                    act.wait_ge(s_mx, b + 1)
                    wait(act, s_pt, b - 1)
                    wait(act, s_yr, b - U + 1)
                    act.activation(pr[:, s, 0, :], bank[2 + s][:, 0:P], ACT.Exp, bias=nmax[:, s, 0:1],
                                   accum_out=rsum[:, q % U, 0:1])
                    act.activation(pr[:, s, 1:3, :].rearrange("p t c -> p (t c)"), bank[2 + s][:, P:3 * P], ACT.Exp,
                                   bias=nmax[:, s, 1:2], accum_out=rsum[:, q % U, 1:2]).then_inc(s_p, 1)
                if has[1]:
                    b, s = k - 1, (q - 1) % 2
                    act.wait_ge(s_pt, b + 1)
                    wait(act, s_y, b - 1)
                    cp(prT[:, s].rearrange("p t c -> p (t c)"), bank[4][:, 0:3 * P]).then_inc(s_pts, 1)
                if has[-1]:
                    copy_z_v(k + 1, q + 1)
                if has[3]:
                    b, s = k - 3, (q - 3) % 2
                    act.wait_ge(s_xht, b + 1)
                    wait(act, s_lg, b - 1)
                    cp(xhT[:, s].rearrange("p t c -> p (t c)"), bank[6][:, 0:T], bias=one_col[:]).then_inc(s_xhts, 1)
                if has[-2]:
                    copy_xT(k + 2, q % 2)
                if has[3]:
                    for t in range(TPB):
                        last = act.activation(x_row(k - 3, t), x_row(k - 3, t), ACT.Identity, bias=zero_col[:],
                                              scale=rr_all[:, bass.ds(k - 3, 1), 0, t])
                    last.then_inc(s_x1, 1)
                if has[2]:
                    b, s = k - 2, q % 2
                    act.wait_ge(s_vv, b + 1)
                    act.activation(lnv[:, s], vv[:, s], ACT.Ln).then_inc(s_ln, 1)
                    act.wait_ge(s_ln, b + 1)
                    act.activation(rr_all[:, bass.ds(b, 1), :, :].rearrange("p a n t -> p (a n) t"), lnv[:, s], ACT.Exp,
                                   scale=-0.5).then_inc(s_rr, 1)
                if known is not None and known < LATE_W:
                    copy_weights(EARLY + known)
            run_steps(act, attend_step, NB + 3, U, 5, 3)
            act.wait_ge(s_gd, 1)
            act.activation(gates[:, :, 1], gd[:], ACT.Exp).then_inc(s_ge, 1)
            act.preload_act_table_set("gelu_and_others")

            def ffn_step(k, q, use, known):
                if known is None or known < NTILE:
                    act.wait_ge(s_gt, k + 1)
                    wait(act, s_h, k - 1)
                    cp(xgT[:, q % 2, :], bank[q % 2][:, 0:P], bias=one_col[:]).then_inc(s_gts, 1)
                if known is None or known >= 3:
                    j, slot = k - 3, (q - 3) % XR
                    act.wait_ge(s_yy, j + 1)
                    wait(act, s_yo[slot], (use if q == 3 else use - 1) * 16)
                    cp(ysb[:, slot, :], bank[4 + (q - 3) % 2][:, 0:P], bias=zero_col[:]).then_inc(s_ys, 1)
                if known is None or 0 <= known - 1 < NTILE:
                    j, s = k - 1, (q - 1) % 2
                    act.wait_ge(s_h, j + 1)
                    wait(act, s_yy, j - 1)
                    act.activation(hs[:, s].rearrange("p h t -> p (h t)"), bank[2 + s][:], ACT.Gelu).then_inc(s_hs, 1)
                if known is None or known >= 3:
                    j, slot = k - 3, (q - 3) % XR
                    act.wait_ge(s_ys, j + 1)
                    act.dma_start(yrows[bass.ds(j * P, P), :], ysb[:, slot]).then_inc(s_yo[slot], 16)
            run_steps(act, ffn_step, NTILE + 3, XR, 8, 3)

            act.preload_act_table_set("natural_log_exp_and_others")

            def rsqrt_act(out_, ln_, neg_var, done):
                act.activation(ln_, neg_var, ACT.Ln, bias=eps_col[:], scale=-1.0).then_inc(s_ln7, 1)
                act.wait_ge(s_ln7, done + 1)
                act.activation(out_, ln_, ACT.Exp, scale=-0.5).then_inc(s_r7, 1)

            def norm(b, t, scale, shift):
                return act.activation(x_row(b, t), x_row(b, t), ACT.Identity, bias=shift, scale=scale)

            act.wait_ge(s_mv, NB0)
            rsqrt_act(r70[:], ln70[:], neg_mv[:, 0:NB0 * TPB, 1], 0)
            act.wait_ge(s_sh70, 1)
            with act.Fori(0, NB0) as b:
                for t in range(TPB):
                    tile = bass.ds(b * TPB + t, 1)
                    last = norm(b, t, r70[:, tile], sh70[:, tile])
                last.then_inc(s_os, 1)

            def norm_step(n, s, use, known):
                b = n + NB0
                mine = neg_mv[:, bass.ds(b * TPB, TPB), :]
                act.wait_ge(s_mv, b + 1)
                rsqrt_act(r7[:, s], ln7[:, s], mine[:, :, 1], n + 1)
                act.wait_ge(s_r7, n + 2)
                for t in range(TPB):
                    last = act.activation(sh7[:, s, t:t + 1], mine[:, t, 0:1], ACT.Identity, bias=zero_col[:],
                                          scale=r7[:, s, t:t + 1])
                last.then_inc(s_sh7, 1)
                act.wait_ge(s_sh7, n + 1)
                for t in range(TPB):
                    last = norm(b, t, r7[:, s, t:t + 1], sh7[:, s, t:t + 1])
                last.then_inc(s_os, 1)
            run_steps(act, norm_step, NB - NB0, 2, 0, 0)

        @block.vector
        def _(v):
            pg = Progress(v, s_dve)

            def op(ins):
                pg.did(ins)

            v.wait_ge(s_const, 1)

            def fold_expert(e, q, use):
                def of_expert(bc):
                    return bc[:, bass.ds(e * P, P)].unsqueeze(1).to_broadcast([P, HC, P])

                w = w1n[:, bass.ds(e, 1)].rearrange("p a k d -> p (a k) d")
                v.wait_ge(s_w[q], use * 32 + 32)
                op(v.tensor_tensor(w1s[:], w, of_expert(ld_bc), ALU.mult))
                op(v.tensor_tensor(w, w, of_expert(ls_bc), ALU.mult))
                pg.settle()
                op(v.tensor_reduce(w1k[:], w1s[:], AXX, ALU.add))
                pg.settle()
                op(v.scalar_tensor_tensor(out=w1k[:], in0=w1k[:], scalar=1.0 / C, in1=b1c[:, bass.ds(e * HC, HC)],
                                          op0=ALU.mult, op1=ALU.add))
                pg.settle()
                v.tensor_tensor(w, w, w1k[:].unsqueeze(2).to_broadcast([P, HC, P]), ALU.add).then_inc(s_w1p, 1)

            def fold_round(r):
                v.wait_ge(s_fold_pe, r + 1)
                if r == 0:
                    op(v.tensor_copy(aAT[:], bank[5][0:R, 0:P]))
                    op(v.tensor_copy(pAT[:], bank[5][0:R, P:2 * P]))
                elif r == 1:
                    op(v.tensor_tensor(wm[:].rearrange("p a c -> p (a c)"), bank[3][:, 0:3 * P],
                                       wa[:].rearrange("p a c -> p (a c)"), ALU.add))
                    op(v.tensor_copy(wpmT[:], bank[2][:, 0:P]))
                elif r == 2:
                    op(v.tensor_copy(wmT[:].rearrange("c (i a) -> c a i", a=3),
                                     bank[4][:, 0:3 * P].rearrange("c (a i) -> c a i", a=3)))
                    op(v.tensor_copy(wp2T[:], bank[2][:, P:2 * P]))
                else:
                    v.wait_ge(s_par, 16 * N_PARAM)
                    op(v.tensor_copy(wn[:].rearrange("p a c -> p (a c)"), bank[5][:, 0:3 * P]))
                    op(v.tensor_tensor(rl_d[:], rlb[:], rls[:], ALU.subtract))
                    pg.settle()
                    op(v.tensor_scalar(rl_bc[:], ones[:], rl_d[:], 1.0 / C, ALU.mult, ALU.mult))
                pg.settle()
                v.sem_inc(s_fold_dve, 1)

            v.wait_ge(s_b1t, 1)
            op(v.tensor_scalar(b1c[:], bank[6][:, 0:E * HC], 1.0 / C, None, ALU.mult))
            v.wait_ge(s_ls, 32)
            op(v.tensor_tensor(ld_bc[:], ld_bc[:], ls_bc[:], ALU.subtract))
            pg.settle()

            def expert_step(e, q, use, known):
                if known is not None:
                    fold_round(known)
                fold_expert(e, q, use)
            LATE_E = 2
            run_steps(v, expert_step, E - LATE_E, 2, 4, 0, progress=pg, per_loop=2 * 4)

            v.wait_ge(s_gram, 1)
            op(v.tensor_scalar(cov[:], bank[7][:, 0:P + 1], 1.0 / NTOK, None, ALU.mult))
            pg.settle()
            v.sem_inc(s_fold_dve, 1)
            v.wait_ge(s_fold_pe, 5)
            pj = bank[3][:, 0:3 * (P + 1)].rearrange("p (g c) -> p g c", g=3)
            for g in range(3):
                op(v.tensor_tensor(scr3[:, g, :], pj[:, g, 0:P], wn[:, g, :], ALU.mult))
            op(v.tensor_copy(bn[:, 2, :], pj[:, :, P]))
            pg.settle()
            op(v.tensor_reduce(bn[:, 0, :], scr3[:], AXX, ALU.add))
            op(v.tensor_tensor(bn[:, 4, :], bn[:, 2, :], bn[:, 2, :], ALU.mult))
            pg.settle()
            op(v.tensor_tensor(bn[:, 0, :], bn[:, 0, :], bn[:, 4, :], ALU.subtract))
            pg.settle()
            v.sem_inc(s_bnv, 1)
            op(v.tensor_scalar(bn[:, 4, :], bn[:, 0, :], -0.5, -0.5 * EPS_BN, ALU.mult, ALU.add))
            v.wait_ge(s_bnr, 1)
            op(v.tensor_tensor(bn[:, 3, :], bn[:, 1, :], bn[:, 1, :], ALU.mult))
            pg.settle()
            op(v.tensor_tensor(bn[:, 3, :], bn[:, 3, :], bn[:, 4, :], ALU.mult))
            pg.settle()
            op(v.scalar_tensor_tensor(out=bn[:, 1, :], in0=bn[:, 3, :], scalar=1.5, in1=bn[:, 1, :],
                                      op0=ALU.add, op1=ALU.mult))
            pg.settle()
            op(v.tensor_tensor(bn[:, 1, :], bn[:, 1, :], gb[:, 0, :], ALU.mult))
            pg.settle()
            op(v.tensor_tensor(bn[:, 3, :], bn[:, 2, :], bn[:, 1, :], ALU.mult))
            pg.settle()
            op(v.tensor_tensor(bn[:, 2, :], gb[:, 1, :], bn[:, 3, :], ALU.subtract))
            pg.settle()
            op(v.tensor_scalar(bn[:, 1:3, 0:1], bn[:, 1:3, 0:1], float(C) ** -0.5, None, ALU.mult))
            pg.settle()
            for g in range(3):
                op(v.tensor_scalar(wn[:, g, :], wn[:, g, :], bn[:, 1, g:g + 1], None, ALU.mult))
            op(v.tensor_scalar(tv_bc[:], ones[:], bn[:, 2, 2:3], None, ALU.mult))
            pg.settle()
            v.sem_inc(s_fold_dve, 1)
            v.wait_ge(s_fold_pe, 6)
            op(v.tensor_copy(MT[:], bank[2][:, 0:P]))
            op(v.tensor_copy(u_z[:], bank[2][:, P:P + 1]))
            op(v.tensor_copy(wvvT[:], bank[3][:, 0:P]))
            op(v.tensor_copy(cv[:], bank[3][:, P:2 * P]))
            op(v.scalar_tensor_tensor(out=RW[:], in0=rwT[:], scalar=rls[:], in1=bank[3][:, 2 * P:2 * P + E],
                                      op0=ALU.mult, op1=ALU.add))
            pg.settle()
            v.sem_inc(s_fold_dve, 1)
            for n in range(3):
                op(v.tensor_copy(cvp[:, n, :], cv[:]))
                pg.settle()
                op(v.tensor_copy(cv3[32 * n:32 * n + 1, :], cvp[32 * n:32 * n + 1, n, :]))
                if n < 2:
                    op(v.tensor_tensor(cv[:], cv[:], cvp[:, n, :], ALU.subtract))
                pg.settle()
            v.sem_inc(s_cv, 1)
            fold_expert(E - 2, 0, E // 2 - 1)

            v.wait_ge(s_cp1, NCH)
            lgb = bank[5][:, T:T + TPB * E].rearrange("p (t e) -> p t e", e=E)
            rkb = bank[7][:, 0:TPB * E].rearrange("p (t e) -> p t e", e=E)

            def attend_step(k, q, use, known):
                has = {d: known is None or 0 <= known - d < NB for d in (0, 1, 2, 3, 4, 5)}
                if known == COUNT0 - 1:
                    with nc.allow_low_precision(reason="whole numbers up to 2 * NT"):
                        v.tensor_reduce(n0_h[:], oh_all[:, 0:NB0 * TPB].rearrange("p t k e -> p e (t k)"),
                                        AXX, ALU.add).then_inc(s_n0, 1)
                b2, q2, s2 = k - 2, (q - 2) % U, q % 2
                b4, s4 = k - 4, q % 2
                b5, q5 = k - 5, (q - 5) % ROWS

                def one_hots(b):
                    return oh_all[:, bass.ds(b * TPB, TPB), :, :]

                if known == COUNT0 + 1:
                    list_first_group()
                if has[0]:
                    b, s = k, q % 2
                    v.wait_ge(s_sc, b + 1)
                    wait(v, s_p, b - 1)
                    v.tensor_reduce(nmax[:, s, 0:1], bank[2 + s][:, 0:P], AXX, ALU.max, negate=True)
                    v.tensor_reduce(nmax[:, s, 1:2], bank[2 + s][:, P:3 * P], AXX, ALU.max,
                                    negate=True).then_inc(s_mx, 1)
                if known == 0:
                    fold_expert(E - 1, 1, E // 2 - 1)
                if has[3]:
                    b, slot = k - 3, (q - 3) % ROWS
                    v.wait_ge(s_rr, b + 1)
                    wait(v, s_scat[slot], (use if q >= 3 else use - 1) * SCAT)
                    for t in range(TPB):
                        last = v.tensor_scalar(xh[:, slot, t, :], x_row(b, t), mv[:, (q - 3) % 2, t, 0:1],
                                               rr_all[:, bass.ds(b, 1), 1, t], ALU.subtract, ALU.mult)
                    last.then_inc(s_xh, 1)
                if has[4]:
                    v.wait_ge(s_lg, b4 + 1)
                if has[2]:
                    v.wait_ge(s_y, b2 + 1)
                    for t in range(TPB):
                        last = v.scalar_tensor_tensor(
                            out=x_row(b2, t), in0=bank[5][:, t * P:(t + 1) * P], scalar=rinv[:, s2, t:t + 1],
                            in1=x_row(b2, t), op0=ALU.mult, op1=ALU.add)
                    last.then_inc(s_yr, 1)
                if has[5]:
                    v.wait_ge(s_rk, b5 + 1)
                    op(v.tensor_tensor(ohr[:], one_hots(b5), rkb.unsqueeze(2).to_broadcast([P, TPB, 2, E]), ALU.mult))
                if has[4]:
                    for t in range(TPB):
                        op(v.max(mx8[:, t, :], lgb[:, t, :]))
                pg.settle()
                if has[5]:
                    with nc.allow_low_precision(reason="whole numbers below 2**24"):
                        op(v.tensor_reduce(pos_all[:, bass.ds(b5 * TPB, TPB), :], ohr[:], AXX, ALU.add))
                        v.tensor_reduce(pos_i[:, q5], ohr[:], AXX, ALU.add).then_inc(s_pos, 1)
                if has[4]:
                    for t in range(TPB):
                        op(v.max_index(ix8[:, t, :], mx8[:, t, :], lgb[:, t, :]))
                    v.tensor_tensor(gd[:, bass.ds(b4 * TPB, TPB)], mx8[:, :, 1], mx8[:, :, 0],
                                    ALU.subtract).then_inc(s_lr, 1)
                if has[2]:
                    if not has[4]:
                        v.wait_ge(s_yr, b2 + 1)
                    for t in range(TPB):
                        op(v.bn_stats(st6[:, t, :], x_row(b2, t)))
                pg.settle()
                if has[4]:
                    op(v.tensor_tensor(one_hots(b4), iota_e[:].unsqueeze(1).unsqueeze(1).to_broadcast([P, TPB, 2, E]),
                                       ix8[:, :, 0:2].unsqueeze(3).to_broadcast([P, TPB, 2, E]), ALU.is_equal))
                if has[1]:
                    v.wait_ge(s_p, k)
                    op(v.reciprocal(rinv[:, (q - 1) % 2, :], rsum[:, (q - 1) % U, :]))
                if has[2]:
                    for t in range(TPB):
                        op(v.bn_aggr(mv[:, s2, t, :], st6[:, t, :]))
                pg.settle()
                if has[4]:
                    v.tensor_tensor(m_sum[:, s4], oh_all[:, bass.ds(b4 * TPB, TPB), 0, :],
                                    oh_all[:, bass.ds(b4 * TPB, TPB), 1, :], ALU.add).then_inc(s_oh, 1)
                if has[2]:
                    op(v.tensor_scalar(vv[:, s2, 0, :], mv[:, s2, :, 1], EPS_POST, None, ALU.add))
                    v.tensor_scalar(vv[:, s2, 1, :], mv[:, s2, :, 1], 1.0 + EPS_FFN, EPS_POST * EPS_FFN, ALU.mult,
                                    ALU.add).then_inc(s_vv, 1)

            def list_first_group():
                v.wait_ge(s_n0t, 1)
                v.wait_ge(s_xhts, COUNT0 - 2)
                op(v.tensor_copy(n0[:], bank[6][:, T:T + E]))
                pg.settle()
                v.sem_inc(s_n0r, 1)
                op(v.tensor_tensor(base[:, 1, 0:E], base[:, 0, 0:E], n0[:], ALU.add))
                op(v.tensor_scalar(tiles_i[:, 0, :], n0[:], P - 1.0, None, ALU.add))
                pg.settle()
                op(v.tensor_copy(ends_i[:], base[0:1, 1, 0:E]))
                count_tiles(0)
                v.sem_inc(s_pad, 1)

            def count_tiles(g):
                op(v.tensor_scalar(tiles_s[:, g, :], tiles_i[:, g, :], P.bit_length() - 1, None,
                                   ALU.logical_shift_right))
                pg.settle()
                op(v.tensor_copy(tiles[:, g, :], tiles_s[:, g, :]))
                pg.settle()
                op(v.tensor_tensor_scan(out=start[:, g, 1:NPART], data0=ones[:, 0:E], data1=tiles[:, g, :],
                                        initial=float(g * NTILE0), op0=ALU.mult, op1=ALU.add))
                pg.settle()
            PER_STEP = 1 + 2 + 1 + 2 + 2 + 1 + 1 + 2 + 1
            run_steps(v, attend_step, NB + 5, ROWS, 3 + ROWS, 8, progress=pg, per_loop=ROWS * PER_STEP)

            v.sem_inc(s_gd, 1)
            v.wait_ge(s_tot, 1)
            ends = bank[7][:, 0:E]
            op(v.scalar_tensor_tensor(out=tiles_i[:, 1, :], in0=ends, scalar=P - 1.0, in1=base[:, 1, 0:E],
                                      op0=ALU.add, op1=ALU.subtract))
            op(v.tensor_scalar(padp[:], ends, part[:], None, ALU.add))
            pg.settle()
            count_tiles(1)
            op(v.tensor_tensor(cmp[:], j_iota[:].unsqueeze(2).to_broadcast([P, 2, 2 * NPART]),
                               start[:].rearrange("p g e -> p (g e)").unsqueeze(1).to_broadcast([P, 2, 2 * NPART]),
                               ALU.is_ge))
            op(v.scalar_tensor_tensor(out=look[:, 0, :], in0=start[:].rearrange("p g e -> p (g e)"),
                                      scalar=-float(P), in1=base[:].rearrange("p g e -> p (g e)"),
                                      op0=ALU.mult, op1=ALU.add))
            pg.settle()
            op(v.tensor_reduce(part_j[:], cmp[:], AXX, ALU.add))
            pg.settle()
            op(v.tensor_tensor(pick[:], part_j[:].unsqueeze(2).to_broadcast([P, 2, 2 * NPART]),
                               g_iota[:].unsqueeze(1).to_broadcast([P, 2, 2 * NPART]), ALU.is_equal))
            pg.settle()
            op(v.tensor_tensor(picked[:], pick[:].unsqueeze(2).to_broadcast([P, 2, 2, 2 * NPART]),
                               look[:].unsqueeze(1).to_broadcast([P, 2, 2, 2 * NPART]), ALU.mult))
            pg.settle()
            op(v.tensor_reduce(tab_p[:], picked[:], AXX, ALU.add))
            pg.settle()
            op(v.scalar_tensor_tensor(out=tab_p[:, :, 0], in0=j_iota[:], scalar=float(P), in1=tab_p[:, :, 0],
                                      op0=ALU.mult, op1=ALU.add))
            pg.settle()
            v.sem_inc(s_tabp, 1)
            v.wait_ge(s_tabt, 1)
            op(v.tensor_copy(tab[:], bank[4][0:1, :].rearrange("p (n j) -> p n j", n=2)[:, :, 0:NTILE]))
            pg.settle()
            v.sem_inc(s_tab, 1)
            v.sem_inc(s_pad, 1)

            def late_routing(part):
                if part == 0:
                    n0_rows = NB0 * TPB * 2
                    for g, rows in enumerate((slice(0, n0_rows), slice(n0_rows, NT * 2))):
                        n = rows.stop - rows.start
                        op(v.tensor_tensor(ohs[:, rows, :], oh_all[:].rearrange("p t k e -> p (t k) e")[:, rows, :],
                                           look[:, 0, g * NPART:g * NPART + E].unsqueeze(1).to_broadcast([P, n, E]),
                                           ALU.mult))
                    v.wait_ge(s_ge, 1)
                    op(v.tensor_scalar(gsum[:], gates[:, :, 1], 1.0, None, ALU.add))
                elif part == 1:
                    op(v.tensor_reduce(yf[:], ohs[:], AXX, ALU.add))
                    op(v.reciprocal(gates[:, :, 0], gsum[:]))
                else:
                    op(v.tensor_tensor(ypos[:].rearrange("p t k -> p (t k)"),
                                       pos_all[:].rearrange("p t k -> p (t k)"), yf[:], ALU.subtract))
                    op(v.tensor_tensor(gates[:, :, 1], gates[:, :, 1], gates[:, :, 0], ALU.mult))
                pg.settle()

            AHEAD = 2

            def fetch_w1(k, q):
                e = v.value_load(tab_e[0:1, bass.ds(k, 1)], min_val=0, max_val=E - 1)
                wait(v, s_h, k - XR + 1)
                v.tensor_copy(w1c[:, q % XR, :], w1T[:, bass.ds(e, 1), :].rearrange("p a h -> p (a h)")
                              ).then_inc(s_w1s, 1)
            for k in range(AHEAD):
                fetch_w1(k, k)

            def ffn_step(k, q, use, known):
                fetch_w1(k + AHEAD, q + AHEAD)
                if known in (1, 2, 3):
                    late_routing(known - 1)
                if known == 3:
                    op(v.tensor_copy(yidx[:].rearrange("p s t c -> p (s t) c"), ypos[:, 0:U * TPB, :]))
                    pg.settle()
                    v.sem_inc(s_ypos, 1)
            K0 = NTILE + 2 - 2 * NB0
            run_steps(v, ffn_step, K0, XR, 4 + K0 % XR, 0)

            def fetch_indices(b, r):
                op(v.tensor_copy(yidx[:, r], ypos[:, bass.ds(b * TPB, TPB), :]))

            def add_rows(b, r, c):
                for t in range(TPB):
                    op(v.scalar_tensor_tensor(
                        out=x_row(b, t), in0=gy[:, r, t, c, :], scalar=gates[:, bass.ds(b * TPB + t, 1), c],
                        in1=x_row(b, t), op0=ALU.mult, op1=ALU.add))

            def combine_half(b, r, use, half, stats, moments):
                pg.settle()
                if half == 0:
                    wait(v, s_gy[r], use * 64 + 64)
                    fetch_indices(b + U, r)
                    if stats:
                        v.sem_inc(s_comb, 1)
                add_rows(b, r, half)
                if half == 0 and moments:
                    store_moments(b - 2)
                if stats:
                    moments_half(b - 1, half)

            def moments_half(b, half):
                for t in range(TPB):
                    if half == 0:
                        op(v.bn_stats(st7[:, t, :], x_row(b, t)))
                    else:
                        op(v.bn_aggr(mv7[:, t, :], st7[:, t, :]))

            def store_moments(b):
                v.tensor_scalar(neg_mv[:, bass.ds(b * TPB, TPB), :], mv7[:], -1.0, None, ALU.mult).then_inc(s_mv, 1)

            v.wait_ge(s_x1, NB)

            def both_step(m, q, use, known):
                if known is None or known + K0 + AHEAD < NTILE:
                    fetch_w1(m + K0 + AHEAD, q + K0 + AHEAD)
                combine_half(use * U + q // 2, q // 2, use, q % 2, known is None or known >= 2,
                             known is None or known >= 4)
            BOTH = 2 * NB0
            run_steps(v, both_step, BOTH, 2 * U, 4 + (BOTH - 4 - 4) % (2 * U), 4, progress=pg, per_loop=U * 9)

            def last_moments(b):
                pg.settle()
                v.sem_inc(s_comb, 1)
                store_moments(b - 1)
                moments_half(b, 0)
                pg.settle()
                moments_half(b, 1)
                pg.settle()
                store_moments(b)

            last_moments(NB0 - 1)
            v.wait_ge(s_r7, 1)
            v.tensor_tensor(sh70[:], neg_mv[:, 0:NB0 * TPB, 0], r70[:], ALU.mult).then_inc(s_sh70, 1)

            def tail_step(n, q, use, known):
                b, r = n + NB0, (q + NB0) % U
                b_use = use + NB0 // U + (q + NB0 % U) // U
                wait(v, s_gy[r], b_use * 64 + 64)
                if known is None or known + U < NB1:
                    fetch_indices(b + U, r)
                for c in range(2):
                    add_rows(b, r, c)
                    pg.settle()
                v.sem_inc(s_comb, 1)
                moments_half(b, 0)
                pg.settle()
                own_wait(v, s_own_dve)
                moments_half(b, 1)
                pg.settle()
                store_moments(b)
            NB1 = NB - NB0
            run_steps(v, tail_step, NB1, U, 2, U, progress=pg, per_loop=U * 9)


NAMES = ("x", "W_attn", "W_proj", "lora_attn_A", "lora_attn_B", "lora_proj_A", "lora_proj_B", "bn_gamma", "bn_beta")
FFN_NAMES = ("router_ln_scale", "router_ln_bias", "router_w", "router_b", "expert_ln_scale", "expert_ln_bias",
             "w1", "b1", "w2", "b2")


def kernel(**inputs):
    import numpy as np
    import concourse.bacc as bacc
    from concourse.bass_utils import run_bass_kernel_spmd

    nc = bacc.Bacc("TRN2", target_bir_lowering=False, num_devices=1)
    arrays, args = {}, []
    for name in ["L0_attn_" + n for n in NAMES] + ["L0_ffn_" + n for n in FFN_NAMES]:
        a = np.ascontiguousarray(inputs[name])
        arrays[name] = a
        args.append(nc.dram_tensor(name, a.shape, mybir.dt.from_np(a.dtype), kind="ExternalInput").ap())
    shape = inputs["L0_attn_x"].shape
    out = nc.dram_tensor("out", shape, F32, kind="ExternalOutput").ap()
    build(nc, *args, out)
    r = run_bass_kernel_spmd(nc, [arrays], core_ids=[0])
    return r.results[0]["out"]
```
